# Optimizing a Trainium2 kernel written in Bass

```python
import numpy as np
import jax
import jax.numpy as jnp

def _softmax(x, axis=-1):
    return jax.nn.softmax(x, axis=axis)

def _gelu(x):
    return jax.nn.gelu(x, approximate=True)

def _silu(x):
    return jax.nn.silu(x)

def _sigmoid(x):
    return jax.nn.sigmoid(x)

def _layernorm(x, axis=-1, eps=1e-05):
    m = jnp.mean(x, axis=axis, keepdims=True)
    v = jnp.var(x, axis=axis, keepdims=True)
    return (x - m) / jnp.sqrt(v + eps)

def _scatter_add(tgt, idx, src, axis=0):
    return tgt.at[idx].add(src)

def _segment_sum(src, seg, n):
    return jax.ops.segment_sum(src, seg, n)
kernel_name = 'mk_metaformer_d1_conv_nchw256_r4_e692e5'

def setup_inputs(seed: int=0):
    np.random.seed(seed)
    _w = jnp.asarray

    def _rec_inputs():
        import jax
        import jax.numpy as jnp
        _gk = jax.random.key(seed)
        x = -0.0003929 + 0.9999 * jax.random.normal(jax.random.fold_in(_gk, 1), (16, 64, 32, 32), jnp.float32)
        return x
    x = _rec_inputs()

    def _L0_conv_setup():
        import jax, jax.numpy as jnp
        import numpy as np

        @jax.custom_vjp
        def bsign(x):
            return jnp.sign(x)

        def _bsign_fwd(x):
            return (jnp.sign(x), x)

        def _bsign_bwd(x, g):
            return (g * (jnp.abs(x) <= 1.0).astype(g.dtype),)
        bsign.defvjp(_bsign_fwd, _bsign_bwd)

        def _conv(x, w):
            return jax.lax.conv_general_dilated(x, w, window_strides=(1, 1), padding='VALID', dimension_numbers=('NCHW', 'OIHW', 'NCHW'))

        def _bn(x, gamma, beta, mean, var, eps=1e-05):
            inv = gamma * jax.lax.rsqrt(var + eps)
            return x * inv[None, :, None, None] + (beta - mean * inv)[None, :, None, None]

        def _pad(x):
            return jnp.pad(x, ((0, 0), (0, 0), (0, 1), (1, 1)))
        key = jax.random.key(seed)
        k0, k1, k2 = jax.random.split(key, 3)
        B, C, H, W = (16, 64, 32, 32)
        x = jax.random.normal(k0, (B, C, H, W), jnp.float32)
        w1 = jax.random.normal(k1, (C, C, 2, 3), jnp.float32) * 0.05
        w2 = jax.random.normal(k2, (C, C, 2, 3), jnp.float32) * 0.05
        ones = jnp.ones((C,), jnp.float32)
        zeros = jnp.zeros((C,), jnp.float32)
        return dict(x=x, w1=w1, gamma1=ones, beta1=zeros, mean1=zeros, var1=ones, w2=w2, gamma2=ones, beta2=zeros, mean2=zeros, var2=ones)
    _L0_conv_all = _L0_conv_setup()
    _L0_conv_in = {k: v for k, v in _L0_conv_all.items() if k in ('w1', 'gamma1', 'beta1', 'mean1', 'var1', 'w2', 'gamma2', 'beta2', 'mean2', 'var2')}
    del _L0_conv_all

    def _L0_ffn_setup():
        import jax, jax.numpy as jnp
        import numpy as np
        D_MODEL = 64
        N_EXPERTS = 16
        HIDDEN = 128
        SCALE = 0.02
        key = jax.random.key(seed)
        ks = jax.random.split(key, 5)
        x = jax.random.normal(ks[0], (4, 2048, D_MODEL), dtype=jnp.float32)
        gate_w = jax.random.normal(ks[1], (D_MODEL, N_EXPERTS), dtype=jnp.float32) * SCALE
        gate_b = jnp.zeros((N_EXPERTS,), dtype=jnp.float32)
        w1 = jax.random.normal(ks[2], (N_EXPERTS, D_MODEL, HIDDEN), dtype=jnp.float32) * SCALE
        w2 = jax.random.normal(ks[3], (N_EXPERTS, D_MODEL, HIDDEN), dtype=jnp.float32) * SCALE
        w3 = jax.random.normal(ks[4], (N_EXPERTS, HIDDEN, D_MODEL), dtype=jnp.float32) * SCALE
        return {'x': x, 'gate_w': gate_w, 'gate_b': gate_b, 'w1': w1, 'w2': w2, 'w3': w3}
    _L0_ffn_all = _L0_ffn_setup()
    _L0_ffn_in = {k: v for k, v in _L0_ffn_all.items() if k in ('gate_w', 'gate_b', 'w1', 'w2', 'w3')}
    del _L0_ffn_all
    return {'x': x, 'L0_conv_w1': _L0_conv_in['w1'], 'L0_conv_gamma1': _L0_conv_in['gamma1'], 'L0_conv_beta1': _L0_conv_in['beta1'], 'L0_conv_mean1': _L0_conv_in['mean1'], 'L0_conv_var1': _L0_conv_in['var1'], 'L0_conv_w2': _L0_conv_in['w2'], 'L0_conv_gamma2': _L0_conv_in['gamma2'], 'L0_conv_beta2': _L0_conv_in['beta2'], 'L0_conv_mean2': _L0_conv_in['mean2'], 'L0_conv_var2': _L0_conv_in['var2'], 'L0_ffn_gate_w': _L0_ffn_in['gate_w'], 'L0_ffn_gate_b': _L0_ffn_in['gate_b'], 'L0_ffn_w1': _L0_ffn_in['w1'], 'L0_ffn_w2': _L0_ffn_in['w2'], 'L0_ffn_w3': _L0_ffn_in['w3']}

def reference(x, L0_conv_w1, L0_conv_gamma1, L0_conv_beta1, L0_conv_mean1, L0_conv_var1, L0_conv_w2, L0_conv_gamma2, L0_conv_beta2, L0_conv_mean2, L0_conv_var2, L0_ffn_gate_w, L0_ffn_gate_b, L0_ffn_w1, L0_ffn_w2, L0_ffn_w3):
    import jax
    import jax.numpy as jnp

    def _L0_conv_ref(x, w1, gamma1, beta1, mean1, var1, w2, gamma2, beta2, mean2, var2):
        import jax, jax.numpy as jnp
        import numpy as np

        @jax.custom_vjp
        def bsign(x):
            return jnp.sign(x)

        def _bsign_fwd(x):
            return (jnp.sign(x), x)

        def _bsign_bwd(x, g):
            return (g * (jnp.abs(x) <= 1.0).astype(g.dtype),)
        bsign.defvjp(_bsign_fwd, _bsign_bwd)

        def _conv(x, w):
            return jax.lax.conv_general_dilated(x, w, window_strides=(1, 1), padding='VALID', dimension_numbers=('NCHW', 'OIHW', 'NCHW'))

        def _bn(x, gamma, beta, mean, var, eps=1e-05):
            inv = gamma * jax.lax.rsqrt(var + eps)
            return x * inv[None, :, None, None] + (beta - mean * inv)[None, :, None, None]

        def _pad(x):
            return jnp.pad(x, ((0, 0), (0, 0), (0, 1), (1, 1)))
        out = _pad(x)
        out = _conv(bsign(out), bsign(w1))
        out = jax.nn.relu(_bn(out, gamma1, beta1, mean1, var1))
        out = _pad(out)
        out = _conv(bsign(out), bsign(w2))
        out = _bn(out, gamma2, beta2, mean2, var2) + x
        return jax.nn.relu(out)

    def _L0_ffn_ref(x, gate_w, gate_b, w1, w2, w3):
        import jax, jax.numpy as jnp
        import numpy as np
        D_MODEL = 64
        N_EXPERTS = 16
        HIDDEN = 128
        SCALE = 0.02
        n_experts = w1.shape[0]
        logits = jnp.einsum('bsd,de->bse', x, gate_w) + gate_b
        probs = jax.nn.softmax(logits, axis=-1)
        top_probs, top_idx = jax.lax.top_k(probs, 2)
        top_probs = top_probs / jnp.sum(top_probs, axis=-1, keepdims=True)
        dispatch = jnp.sum(jax.nn.one_hot(top_idx, n_experts, dtype=x.dtype) * top_probs[..., None], axis=-2)
        h1 = jnp.einsum('bsd,edh->bseh', x, w1)
        h2 = jnp.einsum('bsd,edh->bseh', x, w2)
        hidden = jax.nn.silu(h1) * h2
        expert_out = jnp.einsum('bseh,eho->bseo', hidden, w3)
        return jnp.einsum('bseo,bse->bso', expert_out, dispatch)

    def _gn(v, G=32, eps=1e-05):
        B_, C_, H_, W_ = v.shape
        g = v.reshape(B_, G, C_ // G, H_, W_)
        m = jnp.mean(g, axis=(2, 3, 4), keepdims=True)
        s = jnp.var(g, axis=(2, 3, 4), keepdims=True)
        return ((g - m) / jnp.sqrt(s + eps)).reshape(v.shape)

    def _ln_c(v, eps=1e-06):
        m = jnp.mean(v, axis=1, keepdims=True)
        s = jnp.var(v, axis=1, keepdims=True)
        return (v - m) / jnp.sqrt(s + eps)

    def _ln_t(v, eps=1e-05):
        m = jnp.mean(v, axis=-1, keepdims=True)
        s = jnp.var(v, axis=-1, keepdims=True)
        return (v - m) / jnp.sqrt(s + eps)

    def _to_tokens(v):
        B_, C_, H_, W_ = v.shape
        return v.reshape(B_, C_, H_ * W_).transpose(0, 2, 1)

    def _from_tokens(t, like):
        B_, C_, H_, W_ = like.shape
        return t.transpose(0, 2, 1).reshape(B_, C_, H_, W_)
    x = x + _L0_conv_ref(_ln_c(x), L0_conv_w1, L0_conv_gamma1, L0_conv_beta1, L0_conv_mean1, L0_conv_var1, L0_conv_w2, L0_conv_gamma2, L0_conv_beta2, L0_conv_mean2, L0_conv_var2)
    t = _to_tokens(x)
    t = t + _L0_ffn_ref(_ln_t(t), L0_ffn_gate_w, L0_ffn_gate_b, L0_ffn_w1, L0_ffn_w2, L0_ffn_w3)
    x = _from_tokens(t, x)
    return x

_drawn_inputs = setup_inputs


def setup_inputs(seed=0):
    import zlib

    import numpy as np

    out = dict(_drawn_inputs(seed))
    spreads = {'L0_conv_gamma1': (1.0, 0.2),
     'L0_conv_beta1': (0.0, 0.1),
     'L0_conv_mean1': (0.0, 0.1),
     'L0_conv_var1': (1.0, 0.2),
     'L0_conv_gamma2': (1.0, 0.2),
     'L0_conv_beta2': (0.0, 0.8),
     'L0_conv_mean2': (0.0, 0.8),
     'L0_conv_var2': (1.0, 0.2),
     'L0_ffn_gate_b': (0.0, 0.8)}
    factors = {'L0_ffn_gate_w': 8.0, 'L0_ffn_w1': 8.0, 'L0_ffn_w2': 8.0, 'L0_ffn_w3': 8.0}
    for name, (base, spread) in spreads.items():
        noise = np.random.default_rng([zlib.crc32(name.encode()), seed]).standard_normal(out[name].shape)
        drawn = base * np.exp(spread * noise) if base else spread * noise
        out[name] = jnp.asarray(drawn.astype(out[name].dtype))
    for name, factor in factors.items():
        out[name] = (out[name] * factor).astype(out[name].dtype)
    return out
```

```python
from contextlib import ExitStack

import concourse.bass as bass
from concourse import mybir

ALU = mybir.AluOpType
ACT = mybir.ActivationFunctionType
AX = mybir.AxisListType
F32 = mybir.dt.float32
F32R = mybir.dt.float32r
BF16 = mybir.dt.bfloat16

P = 128
EPS_CONV_LN = 1e-6
EPS_TOKEN_LN = 1e-5
EPS_BN = 1e-5
MASKED = -3.0e38

FRONT = {
    3: [("residual", 0)], 4: [("center", 0), ("residual", 1)], 5: [("center", 1)],
    6: [("var", 0)], 7: [("var", 1)], 8: [("conv1", 0)], 9: [("conv1", 1)],
    10: [("norm", 0)], 11: [("norm", 1)], 12: [("conv2", 0)], 13: [("conv2", 1)],
    15: [("center2", 0)], 16: [("center2", 1)], 17: [("var2", 0)], 18: [("var2", 1)],
    20: [("norm2", 0)], 21: [("norm2", 1)], 22: [("gate", 0)],
    23: [("split", 0), ("back", 0)], 24: [("split", 1)], 25: [("route", 0)],
    26: [("split", 2), ("route", 1)], 28: [("route", 2)], 29: [("route", 3)],
}
TURN = 3
TAIL = {1: [("split", 3), ("dispatch", 0)], 2: [("back", 1)]}
STAGE_STEPS = ("center", "var", "conv1", "norm", "conv2", "center2", "var2", "norm2", "gate", "split", "route")


def metaformer_kernel(nc, x, w1, gamma1, beta1, mean1, var1, w2, gamma2, beta2, mean2, var2,
                      gate_w, gate_b, ffn_w1, ffn_w2, ffn_w3, out):
    B, C, H, W = x.shape
    E, D, HID = ffn_w1.shape
    _, _, KH, KW = w1.shape
    HW = H * W
    PAIRS = B // 2
    CW = 512
    CH = HW // CW
    ROWS = CW // W
    TPC = CW // P
    TILES = CH * TPC
    GROUPS = 2 * CH
    EP = E // 2
    SLOTS = GROUPS * EP
    UNITS = 2 * SLOTS
    ADDS = GROUPS * (EP - 1)
    TAPS = [(i, j) for i in range(KH) for j in range(KW)]
    assert C == D and 2 * C == P and HID == P and CH == 2 and ADDS % 2 == 0 and UNITS % 4 == 0

    x_pairs = x.rearrange("(q two) c h w -> q (two c) (h w)", two=2)
    out_pairs = out.rearrange("(q two) c h w -> q (two c) (h w)", two=2)

    with ExitStack() as ctx:
        def sb(name, shape, dt):
            return ctx.enter_context(nc.sbuf_tensor(name, shape, dt))

        def bank(name, dt=F32, cols=CW):
            return ctx.enter_context(nc.psum_tensor(name, [P, cols], dt))

        def sem(name):
            return ctx.enter_context(nc.semaphore(name))

        ident = sb("ident", [P, P], F32)
        ident_b = sb("ident_b", [P, P], BF16)
        mean_col = sb("mean_col", [P, 2], F32)
        mean_mat = sb("mean_mat", [P, P], F32)
        center_mat = sb("center_mat", [P, P], F32)
        conv_raw = sb("conv_raw", [P, C * KH * KW], F32)
        conv_sign = sb("conv_sign", [P, len(TAPS), 2, C], BF16)
        conv_w = sb("conv_w", [P, 2, len(TAPS), P], BF16)
        bn_raw = sb("bn_raw", [P, 8], F32)
        bn = sb("bn", [P, 2, 2], F32)
        bn_tmp = sb("bn_tmp", [P, 2, 2], F32)
        gate_mat = sb("gate_mat", [P, 2, E], F32)
        gate_bias = sb("gate_bias", [P, E], F32)
        first_rank = sb("first_rank", [P, E], F32)
        rank_int = sb("rank_int", [P, E], mybir.dt.int32)
        up_raw = sb("up_raw", [P, 2, E, HID], F32)
        up_hi = sb("up_hi", [P, 2, E, HID], F32R)
        up_lo = sb("up_lo", [P, 2, E, HID], F32R)
        down_w = sb("down_w", [P, E, D], F32)
        warm = sb("warm", [P, 2], F32)
        start = sb("start", [P, 11], F32)

        x_in = sb("x_in", [P, HW], F32)
        xc = sb("xc", [P, HW], F32)
        sq = sb("sq", [P, HW], F32)
        var_eps = sb("var_eps", [P, 2, CH, TPC, 2], F32)
        rstd_wide = sb("rstd_wide", [P, CH, 2 * TPC, C], F32)
        ones = sb("ones", [P, 2], F32)
        minus_half = sb("minus_half", [P, 2 * TPC], F32)
        rstd = sb("rstd", [P, 2, CH, TPC, 2], F32)
        x_ln = sb("x_ln", [P, HW], F32)
        bn_sum = sb("bn_sum", [P, HW], F32)
        sign1 = sb("sign1", [P, H + 1, W + 2], BF16)
        sign2 = sb("sign2", [P, H + 1, W + 2], BF16)
        x2 = sb("x2", [P, HW], F32)
        x2_keep = sb("x2_keep", [P, HW], F32)
        xn = sb("xn", [P, HW], F32)
        xs = sb("xs", [P, GROUPS, CW], F32R)
        logits = sb("logits", [P, 2 * TILES, E], F32)
        match = sb("match", [P, 2 * TILES, E], F32)
        key = sb("key", [P, 2 * TILES, E], F32)
        pick1 = sb("pick1", [P, 2 * TILES, E], F32)
        pick2 = sb("pick2", [P, 2 * TILES, E], F32)
        top = sb("top", [P, 8, 2 * TILES], F32)
        disp = sb("disp", [P, TILES, 2, E], F32)

        act_s = [sb(f"act_s{i}", [P, CW], F32) for i in range(2)]
        hidden = [sb(f"hidden{i}", [P, CW], F32) for i in range(4)]
        weighted = [sb(f"weighted{i}", [P, TPC, 2, D], F32) for i in range(2)]
        acc = [sb(f"acc{i}", [P, TPC, 2, D], F32) for i in range(2)]
        ffn = sb("ffn", [P, TILES, 2, D], F32)
        out_sb = [sb(f"out_sb{i}", [P, CW], F32) for i in range(CH)]

        up1 = [bank(f"up1_{i}") for i in range(2)]
        up2 = [bank(f"up2_{i}") for i in range(2)]
        down = [bank(f"down_{i}") for i in range(2)]
        misc = [bank(f"misc_{i}") for i in range(2)]

        consts_in = sem("consts_in")
        conv_in = sem("conv_in")
        up_in = sem("up_in")
        x_loaded = sem("x_loaded")
        stored = [sem(f"stored{c}") for c in range(CH)]
        pool_made = sem("pool_made")
        dve_made = sem("dve_made")
        taps_signed = sem("taps_signed")
        taps_turned = sem("taps_turned")
        hi_made = sem("hi_made")
        weights_made = sem("weights_made")
        center_ready, center_read = sem("center_ready"), sem("center_read")
        var_ready, var_read = sem("var_ready"), sem("var_read")
        conv1_ready, conv1_read = sem("conv1_ready"), sem("conv1_read")
        conv2_ready, conv2_read = sem("conv2_ready"), sem("conv2_read")
        center2_ready, center2_read = sem("center2_ready"), sem("center2_read")
        var2_ready, var2_read = sem("var2_ready"), sem("var2_read")
        norm_ready, norm2_ready = sem("norm_ready"), sem("norm2_ready")
        gate_ready, gate_read = sem("gate_ready"), sem("gate_read")
        back_ready = [sem(f"back_ready{c}") for c in range(CH)]
        back_read = [sem(f"back_read{c}") for c in range(CH)]
        rstd_ready, rstd2_ready = sem("rstd_ready"), sem("rstd2_ready")
        powed = sem("powed")
        x_ln_ready = sem("x_ln_ready")
        relu_ready = sem("relu_ready")
        x2_ready = sem("x2_ready")
        x2_kept = sem("x2_kept")
        xn_ready = sem("xn_ready")
        xs_hi_ready = sem("xs_hi_ready")
        xs_ready = sem("xs_ready")
        gap_ready = sem("gap_ready")
        tanh_ready = sem("tanh_ready")
        disp_done = sem("disp_done")
        route_link = sem("route_link")
        up1_ready = sem("up1_ready")
        up2_ready = sem("up2_ready")
        silu_done = sem("silu_done")
        hidden_done = sem("hidden_done")
        down_done = sem("down_done")
        weighted_done = sem("weighted_done")
        added = sem("added")
        ffn_done = sem("ffn_done")

        block = ctx.enter_context(nc.Block())

        def turned(eng, front, slot, finish):
            front()
            for k in range(TURN):
                slot(k, 0, 0, False)
            if PAIRS > 1:
                with eng.Fori(0, PAIRS - 1) as p:
                    for k in range(TURN, SLOTS):
                        slot(k, p, p + 1, True)
                    for k in range(TURN):
                        slot(k, p + 1, p + 1, True)
            for k in range(TURN, SLOTS):
                slot(k, PAIRS - 1, 0, False)
            finish()

        def steps_of(k, looped):
            if k < TURN:
                return TAIL.get(k, []) if looped else []
            return [s for s in FRONT.get(k, []) if looped or s[0] in ("residual", "back")]

        def cols(c):
            return slice(c * CW, (c + 1) * CW)

        @block.sync
        def _(sp):
            sp.dma_start(x_in[:, :], x_pairs[0]).then_inc(x_loaded, 16)
            sp.dma_start(conv_raw[0:C, :], w1.rearrange("o c i j -> o (c i j)")).then_inc(conv_in, 16)
            sp.dma_start(conv_raw[C:P, :], w2.rearrange("o c i j -> o (c i j)")).then_inc(conv_in, 16)
            for m, w in enumerate((ffn_w1, ffn_w2)):
                for half in range(2):
                    sp.dma_start(up_raw[half * D:(half + 1) * D, m, :, :],
                                 w.rearrange("e d h -> d e h")).then_inc(up_in, 16)
            sp.dma_start(down_w[:, :, :], ffn_w3.rearrange("e h d -> h e d")).then_inc(up_in, 16)

            def store(c, p):
                sp.wait_ge(back_read[c], p + 2)
                sp.dma_start(out_pairs[p, :, cols(c)], out_sb[c][:, :]).then_inc(stored[c], 16)

            def load(q):
                sp.wait_ge(x2_ready, CH * q)
                sp.dma_start(x_in[:, :], x_pairs[q]).then_inc(x_loaded, 16)

            load(1)
            with sp.Fori(0, PAIRS - 2) as p:
                load(p + 2)
                for c in range(CH):
                    store(c, p)
            for p in range(PAIRS - 2, PAIRS):
                for c in range(CH):
                    store(c, p)
            for c in range(CH):
                sp.wait_ge(stored[c], 16 * PAIRS + 16)

        @block.gpsimd
        def _(pool):
            for i, v in enumerate((gamma1, beta1, mean1, var1, gamma2, beta2, mean2, var2)):
                for half in range(2):
                    pool.dma_start(bn_raw[half * C:(half + 1) * C, i:i + 1],
                                   v.rearrange("(c one) -> c one", one=1)).then_inc(consts_in, 16)
            pool.memset(gate_mat[:, :, :], 0.0).then_inc(pool_made, 1)
            pool.memset(ident[:, :], 0.0).then_inc(pool_made, 1)
            pool.memset(mean_mat[:, :], 0.0).then_inc(pool_made, 1)
            pool.memset(mean_col[:, :], 0.0).then_inc(pool_made, 1)
            pool.memset(minus_half[:, :], -0.5).then_inc(pool_made, 1)
            pool.memset(ones[:, :], 1.0).then_inc(pool_made, 1)
            pool.memset(conv_w[:, :, :, :], 0.0).then_inc(pool_made, 1)
            pool.iota(rank_int[:, :], [[-1, E]], base=E, channel_multiplier=0).then_inc(pool_made, 1)
            pool.wait_ge(pool_made, 8)
            for half in range(2):
                pool.wait_ge(pool_made, 8 + 2 * half)
                pool.dma_start(gate_mat[half * D:(half + 1) * D, half, :], gate_w).then_inc(consts_in, 16)
                pool.memset(mean_mat[half * C:(half + 1) * C, half * C:(half + 1) * C], 1.0 / C)\
                    .then_inc(pool_made, 1)
                pool.memset(mean_col[half * C:(half + 1) * C, half:half + 1], 1.0 / C).then_inc(pool_made, 1)
            pool.dma_start(gate_bias[:, :], gate_b.partition_broadcast(P)).then_inc(consts_in, 16)
            pool.wait_ge(pool_made, 12)
            pool.affine_select(out=ident[:, :], in_=ident[:, :], compare_op=ALU.not_equal, fill=1.0,
                               base=0, pattern=[[-1, P]], channel_multiplier=1).then_inc(pool_made, 1)
            pool.wait_ge(consts_in, 16 * 19)
            pool.wait_ge(dve_made, 7)
            pool.tensor_tensor(bn_tmp[:, :, 0:1], bn_tmp[:, :, 0:1],
                               minus_half[:, 0:2].unsqueeze(2), ALU.pow).then_inc(pool_made, 1)

            def step(name, c, p, q):
                if name in ("var", "var2"):
                    n = 0 if name == "var" else 1
                    pool.wait_ge((var_read, var2_read)[n], CH * q + c + 1)
                    pool.tensor_tensor(rstd[:, n, c, :, :], var_eps[:, n, c, :, :],
                                       minus_half[:, :].rearrange("p (t a) -> p t a", a=2), ALU.pow).then_inc(powed, 1)
                    pool.wait_ge(powed, 2 * CH * q + CH * n + c + 1)
                    pool.tensor_tensor(rstd_wide[:, c, :, :],
                                       rstd[:, n, c, :, :].rearrange("p t a -> p (t a)").unsqueeze(2)
                                       .to_broadcast([P, 2 * TPC, C]),
                                       ones[:, 0:1].unsqueeze(2).to_broadcast([P, 2 * TPC, C]), ALU.mult)\
                        .then_inc((rstd_ready, rstd2_ready)[n], 1)
                elif name == "conv2":
                    pool.wait_ge(x2_kept, CH * q)
                    pool.wait_ge(relu_ready, CH * q + c + 1)
                    pool.tensor_tensor(x2[:, cols(c)], x_in[:, cols(c)], bn_sum[:, cols(c)], ALU.add)\
                        .then_inc(x2_ready, 1)

            def front():
                for name in STAGE_STEPS:
                    for c in range(CH):
                        step(name, c, 0, 0)

            def slot(k, p, q, looped):
                group, ep = k // EP, k % EP
                if ep > 0:
                    n = (EP - 1) * group + ep - 1
                    pool.wait_ge(weighted_done, SLOTS * p + k + 3)
                    if ep > 1:
                        pool.wait_ge(added, ADDS * p + n + 2)
                    pool.tensor_tensor(acc[group % 2][:, :, :, :], acc[group % 2][:, :, :, :],
                                       weighted[n % 2][:, :, :, :], ALU.add).then_inc(added, 1)
                if ep == EP - 1:
                    chunk, image = group // 2, group % 2
                    pool.wait_ge(back_ready[chunk], p + 1)
                    pool.wait_ge(added, ADDS * p + (EP - 1) * (group + 1) + 2)
                    pool.tensor_tensor(ffn[:, chunk * TPC:(chunk + 1) * TPC, image, :],
                                       acc[group % 2][:, :, 0, :], acc[group % 2][:, :, 1, :], ALU.add)\
                        .then_inc(ffn_done, 1)
                for name, c in steps_of(k, looped):
                    step(name, c, p - 1 if (name, c) == ("back", 1) else p, q)

            turned(pool, front, slot, lambda: None)

        @block.scalar
        def _(act):
            act.wait_ge(dve_made, 1)
            act.activation(warm[:, 1:2], warm[:, 0:1], ACT.Silu).then_inc(silu_done, 2)
            act.wait_ge(dve_made, 11)
            act.wait_ge(conv_in, 32)
            for half in range(2):
                act.activation(conv_sign[:, :, half, :],
                               conv_raw[:, :].rearrange("p (c t) -> p t c", t=len(TAPS)), ACT.Sign)\
                    .then_inc(taps_signed, 1)

            def make_hi():
                act.wait_ge(up_in, 16 * 5)
                for m in range(2):
                    act.activation(up_hi[:, m, :, :], up_raw[:, m, :, :], ACT.Copy).then_inc(hi_made, 1)

            def step(name, c, p, q):
                if name == "residual":
                    act.wait_ge(back_read[c], p + 1)
                    act.wait_ge(x2_ready, CH * (p + 1))
                    act.activation(x2_keep[:, cols(c)], x2[:, cols(c)], ACT.Copy).then_inc(x2_kept, 1)
                elif name == "center":
                    act.wait_ge(center_ready, CH * q + c + 1)
                    act.wait_ge(xn_ready, CH * q)
                    act.activation(sq[:, cols(c)], misc[c][:, :], ACT.Square)
                    act.activation(sign1[:, c * ROWS:(c + 1) * ROWS, 1:W + 1],
                                   misc[c][:, :].rearrange("p (h w) -> p h w", w=W), ACT.Sign)
                    act.activation(xc[:, cols(c)], misc[c][:, :], ACT.Copy).then_inc(center_read, 1)
                elif name == "conv2":
                    act.wait_ge(conv2_read, CH * q + c + 1)
                    act.activation(bn_sum[:, cols(c)], bn_sum[:, cols(c)], ACT.Relu, bias=bn[:, 1, 1:2])\
                        .then_inc(relu_ready, 1)
                elif name == "center2":
                    act.wait_ge(center2_ready, CH * q + c + 1)
                    act.activation(sq[:, cols(c)], misc[c][:, :], ACT.Square)
                    act.activation(xc[:, cols(c)], misc[c][:, :], ACT.Copy).then_inc(center2_read, 1)
                elif name == "split":
                    chunk, image = c // 2, c % 2
                    rows = slice(image * D, (image + 1) * D)
                    act.wait_ge(xn_ready, CH * (q + 1))
                    if not isinstance(q, int) or q > 0:
                        act.wait_ge(up2_ready, UNITS * q - UNITS + 2 * EP * (c + 1))
                    act.activation(xs[rows, c, :], xn[rows, cols(chunk)], ACT.Copy).then_inc(xs_hi_ready, 1)
                elif name == "route" and c == 1:
                    act.wait_ge(gap_ready, q + 1)
                    act.activation(top[:, 5, :], top[:, 4, :], ACT.Tanh, scale=0.5).then_inc(tanh_ready, 1)

            def front():
                for name in STAGE_STEPS:
                    for c in range(4 if name in ("split", "route") else CH):
                        step(name, c, 0, 0)
                    if name == "conv1":
                        make_hi()

            def slot(k, p, q, looped):
                for u in (2 * k, 2 * k + 1):
                    act.wait_ge(up1_ready, UNITS * p + u + 1)
                    act.wait_ge(hidden_done, UNITS * p + u + 1)
                    act.activation(act_s[u % 2][:, :], up1[u % 2][:, :], ACT.Silu).then_inc(silu_done, 1)
                for name, c in steps_of(k, looped):
                    step(name, c, p - 1 if (name, c) == ("back", 1) else p, q)

            turned(act, front, slot, lambda: None)

        @block.tensor
        def _(pe):
            pe.wait_ge(pool_made, 13)
            pe.wait_ge(dve_made, 6)

            def transpose_taps():
                pe.wait_ge(taps_signed, 2)
                turned_taps = misc[1][:, :].bitcast(BF16)
                for t in range(len(TAPS)):
                    last = pe.transpose(turned_taps[:, t * P:(t + 1) * P],
                                        conv_sign[:, t, :, :].rearrange("p a c -> p (a c)"), ident_b[:, :])
                last.then_inc(taps_turned, 1)

            def conv(c, which, image):
                for t, (i, j) in enumerate(TAPS):
                    last = pe.matmul(misc[c][:, :], conv_w[:, which, t, :],
                                     image[:, c * ROWS + i:(c + 1) * ROWS + i, j:j + W],
                                     start=(t == 0), stop=(t == len(TAPS) - 1))
                return last

            def step(name, c, p, q):
                if name == "center":
                    pe.wait_ge(x_loaded, 16 * (q + 1))
                    pe.wait_ge(gate_read, q)
                    if not isinstance(q, int):
                        pe.wait_ge(back_read[c], p + 1)
                    pe.matmul(misc[c][:, :], center_mat[:, :], x_in[:, cols(c)], start=True, stop=True)\
                        .then_inc(center_ready, 1)
                elif name in ("var", "var2"):
                    n = 0 if name == "var" else 1
                    pe.wait_ge((center_read, center2_read)[n], CH * q + c + 1)
                    for t in range(TPC):
                        last = pe.matmul(misc[c][:, 2 * t:2 * t + 2],
                                         sq[:, c * CW + t * P:c * CW + (t + 1) * P], mean_col[:, :],
                                         start=True, stop=True)
                    last.then_inc((var_ready, var2_ready)[n], 1)
                elif name in ("norm", "norm2"):
                    n = 0 if name == "norm" else 1
                    pe.wait_ge((conv1_read, var2_read)[n], CH * q + c + 1)
                    pe.wait_ge((rstd_ready, rstd2_ready)[n], CH * q + c + 1)
                    for t in range(TPC):
                        last = pe.transpose(misc[c][:, t * P:(t + 1) * P],
                                            rstd_wide[:, c, 2 * t:2 * t + 2, :].rearrange("p a c -> p (a c)"),
                                            ident[:, :])
                    last.then_inc((norm_ready, norm2_ready)[n], 1)
                elif name == "conv1":
                    pe.wait_ge(var_read, CH * q + c + 1)
                    pe.wait_ge(center_read, CH * (q + 1))
                    conv(c, 0, sign1).then_inc(conv1_ready, 1)
                elif name == "conv2":
                    pe.wait_ge(conv1_read, CH * (q + 1))
                    pe.wait_ge(x_ln_ready, CH * q + c + 1)
                    conv(c, 1, sign2).then_inc(conv2_ready, 1)
                elif name == "center2":
                    pe.wait_ge(conv2_read, CH * q + c + 1)
                    pe.wait_ge(x2_ready, CH * q + c + 1)
                    pe.matmul(misc[c][:, :], center_mat[:, :], x2[:, cols(c)], start=True, stop=True)\
                        .then_inc(center2_ready, 1)
                elif name == "gate" and c == 0:
                    pe.wait_ge(xn_ready, CH * (q + 1))
                    for j in range(TILES):
                        last = pe.matmul(misc[0][:, j * 2 * E:(j + 1) * 2 * E], xn[:, j * P:(j + 1) * P],
                                         gate_mat[:, :, :].rearrange("p a e -> p (a e)"), start=True, stop=True)
                    last.then_inc(gate_ready, 1)
                elif name == "back":
                    pe.wait_ge(ffn_done, GROUPS * p + 2 * (c + 1) + 2)
                    if c == 0:
                        pe.wait_ge(gate_read, q + 1 if not isinstance(q, int) else PAIRS)
                    else:
                        pe.wait_ge(xn_ready, CH * (q + 1) if not isinstance(q, int) else CH * PAIRS)
                    for t in range(TPC):
                        last = pe.transpose(misc[c][:, t * P:(t + 1) * P],
                                            ffn[:, c * TPC + t, :, :].rearrange("p a d -> p (a d)"), ident[:, :])
                    last.then_inc(back_ready[c], 1)

            def front():
                for name in STAGE_STEPS:
                    for c in range(CH):
                        step(name, c, 0, 0)
                    if name == "center":
                        pe.wait_ge(center_read, CH)
                        transpose_taps()
                        pe.wait_ge(weights_made, 1)

            def down_product(u, p):
                k, e = u // 2, u % E
                pe.wait_ge(hidden_done, UNITS * p + u + 3)
                if u % 2 == 0:
                    pe.wait_ge(weighted_done, SLOTS * p + k + 1)
                for t in range(TPC):
                    last = pe.matmul(down[k % 2][:, (2 * t + u % 2) * D:(2 * t + u % 2 + 1) * D],
                                     hidden[u % 4][:, t * P:(t + 1) * P], down_w[:, e, :],
                                     start=True, stop=True)
                last.then_inc(down_done, 1)

            def slot(k, p, q, looped):
                group = k // EP
                if k == 0 and isinstance(p, int):
                    pe.wait_ge(weights_made, 3)
                if k % EP == 0:
                    pe.wait_ge(xs_ready, GROUPS * p + group + 1)
                for u in (2 * k, 2 * k + 1):
                    e = u % E
                    for m, (banks, free, ready) in enumerate(((up1, silu_done, up1_ready),
                                                              (up2, hidden_done, up2_ready))):
                        pe.wait_ge(free, UNITS * p + u + 1)
                        pe.matmul(banks[u % 2][:, :], up_hi[:, m, e, :], xs[:, group, :], start=True, stop=False)
                        pe.matmul(banks[u % 2][:, :], up_lo[:, m, e, :], xs[:, group, :], start=False, stop=True)\
                            .then_inc(ready, 1)
                    if u >= 2:
                        down_product(u - 2, p)
                    elif not isinstance(p, int):
                        down_product(u - 2 + UNITS, p - 1)
                for name, c in steps_of(k, looped):
                    step(name, c, p - 1 if (name, c) == ("back", 1) else p, q)

            def finish():
                for u in (UNITS - 2, UNITS - 1):
                    down_product(u, PAIRS - 1)
                step("back", 1, PAIRS - 1, 0)

            turned(pe, front, slot, finish)

        @block.vector
        def _(dve):
            dve.memset(warm[:, :], 0.0).then_inc(dve_made, 1)
            dve.memset(sign1[:, :, :], 0.0).then_inc(dve_made, 1)
            dve.memset(sign2[:, :, :], 0.0).then_inc(dve_made, 1)
            for i, (free, count) in enumerate(((hidden_done, 2), (down_done, 4), (added, 2),
                                               (weighted_done, 2), (ffn_done, 2),
                                               (back_ready[0], 1), (back_ready[1], 1), (back_read[0], 1),
                                               (back_read[1], 1), (stored[0], 16), (stored[1], 16))):
                dve.memset(start[:, i:i + 1], 0.0).then_inc(free, count)
            dve.wait_ge(pool_made, 13)
            dve.tensor_copy(ident_b[:, :], ident[:, :]).then_inc(dve_made, 1)
            dve.tensor_tensor(center_mat[:, :], ident[:, :], mean_mat[:, :], ALU.subtract).then_inc(dve_made, 1)
            dve.tensor_copy(first_rank[:, :], rank_int[:, :]).then_inc(dve_made, 1)
            dve.wait_ge(consts_in, 16 * 19)
            raw = bn_raw[:, :].rearrange("p (k v) -> p k v", k=2)
            dve.tensor_scalar(bn_tmp[:, :, 0:1], raw[:, :, 3:4], EPS_BN, None, ALU.add).then_inc(dve_made, 1)
            dve.wait_ge(pool_made, 14)
            dve.tensor_tensor(bn[:, :, 0:1], bn_tmp[:, :, 0:1], raw[:, :, 0:1], ALU.mult).then_inc(dve_made, 1)
            dve.wait_ge(dve_made, 8)
            dve.tensor_tensor(bn_tmp[:, :, 1:2], raw[:, :, 2:3], bn[:, :, 0:1], ALU.mult).then_inc(dve_made, 1)
            dve.wait_ge(dve_made, 9)
            dve.tensor_tensor(bn[:, 0, 1:2], bn_tmp[:, 0, 1:2], raw[:, 0, 1:2], ALU.subtract).then_inc(dve_made, 1)
            dve.tensor_tensor(bn[:, 1, 1:2], raw[:, 1, 1:2], bn_tmp[:, 1, 1:2], ALU.subtract).then_inc(dve_made, 1)
            dve.wait_ge(dve_made, 11)

            def place_taps():
                dve.wait_ge(taps_turned, 1)
                turned_taps = misc[1][:, :].bitcast(BF16)[:, 0:len(TAPS) * P]
                turned_taps = turned_taps.rearrange("p (t k o) -> p t k o", t=len(TAPS), k=2)
                for half in range(2):
                    rows = slice(half * C, (half + 1) * C)
                    for k in range(2):
                        last = dve.tensor_copy(conv_w[rows, k, :, rows], turned_taps[rows, :, k, :])
                last.then_inc(weights_made, 1)

            def make_lo():
                for m in range(2):
                    dve.wait_ge(hi_made, m + 1)
                    dve.tensor_tensor(up_lo[:, m, :, :], up_raw[:, m, :, :], up_hi[:, m, :, :].bitcast(F32),
                                      ALU.subtract).then_inc(weights_made, 1)

            LINKS = 15

            def spread(a):
                return a.unsqueeze(2).to_broadcast([P, 2 * TILES, E])

            def ranks():
                return first_rank[:, :].unsqueeze(1).to_broadcast([P, 2 * TILES, E])

            def pick_first(values, best, pick, q, at):
                dve.tensor_reduce(best, values, AX.X, ALU.max).then_inc(route_link, 1)
                dve.wait_ge(route_link, LINKS * q + at)
                dve.tensor_tensor(match[:, :, :], values, spread(best), ALU.is_equal).then_inc(route_link, 1)
                dve.wait_ge(route_link, LINKS * q + at + 1)
                dve.tensor_tensor(key[:, :, :], match[:, :, :], ranks(), ALU.mult).then_inc(route_link, 1)
                dve.wait_ge(route_link, LINKS * q + at + 2)
                dve.tensor_reduce(top[:, 7, :], key[:, :, :], AX.X, ALU.max).then_inc(route_link, 1)
                dve.wait_ge(route_link, LINKS * q + at + 3)
                dve.tensor_tensor(pick[:, :, :], key[:, :, :], spread(top[:, 7, :]), ALU.is_equal).then_inc(route_link, 1)

            def step(name, c, p, q):
                if name in ("var", "var2"):
                    n = 0 if name == "var" else 1
                    dve.wait_ge((var_ready, var2_ready)[n], CH * q + c + 1)
                    dve.tensor_scalar(var_eps[:, n, c, :, :],
                                      misc[c][:, 0:2 * TPC].rearrange("p (t a) -> p t a", a=2),
                                      (EPS_CONV_LN, EPS_TOKEN_LN)[n], None, ALU.add)\
                        .then_inc((var_read, var2_read)[n], 1)
                elif name == "norm":
                    dve.wait_ge(norm_ready, CH * q + c + 1)
                    dve.tensor_tensor(x_ln[:, cols(c)], misc[c][:, :], xc[:, cols(c)], ALU.mult)\
                        .then_inc(x_ln_ready, 1)
                elif name == "norm2":
                    dve.wait_ge(norm2_ready, CH * q + c + 1)
                    dve.tensor_tensor(xn[:, cols(c)], misc[c][:, :], xc[:, cols(c)], ALU.mult)\
                        .then_inc(xn_ready, 1)
                elif name == "conv1":
                    dve.wait_ge(conv1_ready, CH * q + c + 1)
                    dve.tensor_scalar(sign2[:, c * ROWS:(c + 1) * ROWS, 1:W + 1],
                                      misc[c][:, :].rearrange("p (h w) -> p h w", w=W),
                                      bn[:, 0, 0:1], bn[:, 0, 1:2], ALU.mult, ALU.is_gt).then_inc(conv1_read, 1)
                elif name == "conv2":
                    dve.wait_ge(conv2_ready, CH * q + c + 1)
                    dve.wait_ge(x_ln_ready, CH * q + c + 1)
                    dve.scalar_tensor_tensor(out=bn_sum[:, cols(c)], in0=misc[c][:, :], scalar=bn[:, 1, 0:1],
                                             in1=x_ln[:, cols(c)], op0=ALU.mult, op1=ALU.add)\
                        .then_inc(conv2_read, 1)
                elif name == "gate" and c == 0:
                    dve.wait_ge(gate_ready, q + 1)
                    dve.tensor_tensor(logits[:, :, :],
                                      misc[0][:, 0:2 * TILES * E].rearrange("p (t e) -> p t e", e=E),
                                      gate_bias[:, :].unsqueeze(1).to_broadcast([P, 2 * TILES, E]), ALU.add)\
                        .then_inc(gate_read, 1)
                elif name == "split":
                    chunk, image = c // 2, c % 2
                    rows = slice(image * D, (image + 1) * D)
                    other = slice((1 - image) * D, (2 - image) * D)
                    dve.wait_ge(xs_hi_ready, GROUPS * q + c + 1)
                    dve.tensor_tensor(xs[other, c, :], xn[rows, cols(chunk)], xs[rows, c, :].bitcast(F32),
                                      ALU.subtract).then_inc(xs_ready, 1)
                elif name == "route" and c == 0:
                    dve.wait_ge(gate_read, q + 1)
                    pick_first(logits[:, :, :], top[:, 0, :], pick1, q, 1)
                elif name == "route" and c == 1:
                    dve.wait_ge(route_link, LINKS * q + 5)
                    dve.scalar_tensor_tensor(out=logits[:, :, :], in0=pick1[:, :, :], scalar=MASKED,
                                             in1=logits[:, :, :], op0=ALU.mult, op1=ALU.add)\
                        .then_inc(route_link, 1)
                    dve.wait_ge(route_link, LINKS * q + 6)
                    pick_first(logits[:, :, :], top[:, 1, :], pick2, q, 7)
                    dve.tensor_tensor(top[:, 4, :], top[:, 0, :], top[:, 1, :], ALU.subtract).then_inc(gap_ready, 1)
                elif name == "route" and c == 2:
                    dve.wait_ge(tanh_ready, q + 1)
                    dve.tensor_scalar(top[:, 2, :], top[:, 5, :], 0.5, 0.5, ALU.mult, ALU.add).then_inc(route_link, 1)
                    dve.tensor_scalar(top[:, 3, :], top[:, 5, :], -0.5, 0.5, ALU.mult, ALU.add)\
                        .then_inc(route_link, 1)
                elif name == "route" and c == 3:
                    dve.wait_ge(route_link, LINKS * q + 13)
                    dve.tensor_tensor(pick1[:, :, :], pick1[:, :, :], spread(top[:, 2, :]), ALU.mult)\
                        .then_inc(route_link, 1)
                    dve.tensor_tensor(pick2[:, :, :], pick2[:, :, :], spread(top[:, 3, :]), ALU.mult)\
                        .then_inc(route_link, 1)
                elif name == "dispatch":
                    dve.wait_ge(route_link, LINKS * q + LINKS)
                    dve.wait_ge(weighted_done, SLOTS * q + 2)
                    dve.tensor_tensor(disp[:, :, :, :].rearrange("p t a e -> p (t a) e"), pick1[:, :, :],
                                      pick2[:, :, :], ALU.add).then_inc(disp_done, 1)
                elif name == "back":
                    dve.wait_ge(back_ready[c], p + 2)
                    dve.wait_ge(x2_kept, CH * p + c + 1)
                    dve.wait_ge(stored[c], 16 * p + 16)
                    dve.tensor_tensor(out_sb[c][:, :], misc[c][:, :], x2_keep[:, cols(c)], ALU.add)\
                        .then_inc(back_read[c], 1)

            def front():
                for name in STAGE_STEPS:
                    for c in range(4 if name in ("split", "route") else CH):
                        step(name, c, 0, 0)
                    if name == "center":
                        place_taps()
                    if name == "conv1":
                        make_lo()
                step("dispatch", 0, 0, 0)

            def weigh(k, p):
                group, ep = k // EP, k % EP
                chunk, image = group // 2, group % 2
                dve.wait_ge(down_done, UNITS * p + 2 * k + 6)
                weights = disp[:, chunk * TPC:(chunk + 1) * TPC, image, 2 * ep:2 * ep + 2]
                weights = weights.unsqueeze(3).to_broadcast([P, TPC, 2, D])
                if k == 0:
                    dve.wait_ge(disp_done, p + 1)
                if ep == 0:
                    dve.wait_ge(ffn_done, GROUPS * p + group + 1)
                    dst = acc[group % 2]
                else:
                    n = (EP - 1) * group + ep - 1
                    dve.wait_ge(added, ADDS * p + n + 1)
                    dst = weighted[n % 2]
                dve.tensor_tensor(dst[:, :, :, :], down[k % 2][:, :].rearrange("p (t a d) -> p t a d", a=2, d=D),
                                  weights, ALU.mult).then_inc(weighted_done, 1)

            def slot(k, p, q, looped):
                for u in (2 * k, 2 * k + 1):
                    dve.wait_ge(silu_done, UNITS * p + u + 3)
                    dve.wait_ge(up2_ready, UNITS * p + u + 1)
                    dve.wait_ge(down_done, UNITS * p + u + 1)
                    dve.tensor_tensor(hidden[u % 4][:, :], act_s[u % 2][:, :], up2[u % 2][:, :], ALU.mult)\
                        .then_inc(hidden_done, 1)
                for name, c in steps_of(k, looped):
                    if name == "split" and c == 3 or name == "dispatch":
                        continue
                    step(name, c, p - 1 if (name, c) == ("back", 1) else p, q)
                if k == 0 and not isinstance(p, int):
                    weigh(SLOTS - 1, p - 1)
                elif k > 0:
                    if k == 1 and looped:
                        step("split", 3, p, q)
                        step("dispatch", 0, p, q)
                    weigh(k - 1, p)

            def finish():
                weigh(SLOTS - 1, PAIRS - 1)
                step("back", 1, PAIRS - 1, 0)

            turned(dve, front, slot, finish)


_INS = ["x", "L0_conv_w1", "L0_conv_gamma1", "L0_conv_beta1", "L0_conv_mean1", "L0_conv_var1",
        "L0_conv_w2", "L0_conv_gamma2", "L0_conv_beta2", "L0_conv_mean2", "L0_conv_var2",
        "L0_ffn_gate_w", "L0_ffn_gate_b", "L0_ffn_w1", "L0_ffn_w2", "L0_ffn_w3"]


def kernel(**inputs):
    import numpy as _np
    import concourse.bacc as _bacc
    from concourse import mybir as _mybir
    from concourse.bass_utils import run_bass_kernel_spmd as _run

    nc = _bacc.Bacc("TRN2", target_bir_lowering=False, num_devices=1)
    arrays, args = {}, []
    for name in _INS:
        a = _np.ascontiguousarray(inputs[name])
        arrays[f"in_{name}"] = a
        args.append(nc.dram_tensor(f"in_{name}", a.shape, _mybir.dt.from_np(a.dtype), kind="ExternalInput").ap())
    shape = arrays["in_x"].shape
    args.append(nc.dram_tensor("out_0", shape, _mybir.dt.float32, kind="ExternalOutput").ap())
    metaformer_kernel(nc, *args)
    r = _run(nc, [arrays], core_ids=[0])
    return r.results[0]["out_0"]
```

```python
from contextlib import ExitStack

import concourse.bass as bass
from concourse import mybir

ALU = mybir.AluOpType
ACT = mybir.ActivationFunctionType
AX = mybir.AxisListType
F32 = mybir.dt.float32
F32R = mybir.dt.float32r
BF16 = mybir.dt.bfloat16
F16 = mybir.dt.float16
U32 = mybir.dt.uint32

P = 128
EPS_CONV_LN = 1e-6
EPS_TOKEN_LN = 1e-5
EPS_BN = 1e-5
MASKED = -3.0e38
LEAST_WEIGHT = 2.0 ** -30
EXPONENT_BITS = 0x7F800000

PLAN = {
    5: [("residual", 0), ("center", 0)], 6: [("residual", 1), ("center", 1)],
    7: [("var", 0)], 8: [("var", 1)], 9: [("conv1", 0)], 10: [("conv1", 1)],
    11: [("norm", 0)], 12: [("norm", 1)], 13: [("conv2", 0)], 14: [("conv2", 1)],
    17: [("center2", 0)], 18: [("center2", 1)], 19: [("var2", 0)], 20: [("var2", 1)],
    22: [("norm2", 0)], 23: [("norm2", 1)], 24: [("gate", 0)],
    25: [("split", 0), ("back", 0)], 26: [("split", 1), ("route", 0)], 27: [("split", 2), ("route", 1)],
    28: [("route", 2)], 29: [("route", 3)], 30: [("route", 4)], 31: [("route", 5)],
    32: [("split", 3)], 33: [("route", 6)], 34: [("route", 7)], 36: [("back", 1)],
}
LATER = {
    "TensorE": {},
    "VectorE": {"split": 1},
    "ScalarE": {"var": 2, "var2": 2, "conv2": 1},
    "Pool": {"var": 1, "var2": 1, "conv2": 2},
}
TURN = 5
ROUTE_PARTS = 8
HI_LAG = 1
LO_LAG = 2
DOWN_LAG = 4
WEIGH_LAG = 3
RING = 8
STAGE_STEPS = ("center", "var", "conv1", "norm", "conv2", "center2", "var2", "norm2", "gate", "split", "route")


def metaformer_kernel(nc, x, w1, gamma1, beta1, mean1, var1, w2, gamma2, beta2, mean2, var2,
                      gate_w, gate_b, ffn_w1, ffn_w2, ffn_w3, out):
    B, C, H, W = x.shape
    E, D, HID = ffn_w1.shape
    _, _, KH, KW = w1.shape
    HW = H * W
    PAIRS = B // 2
    CW = 512
    CH = HW // CW
    ROWS = CW // W
    TPC = CW // P
    TILES = CH * TPC
    GROUPS = 2 * CH
    EP = E // 2
    SLOTS = GROUPS * EP
    UNITS = 2 * SLOTS
    ADDS = GROUPS * (EP - 1)
    TAPS = [(i, j) for i in range(KH) for j in range(KW)]
    assert C == D and 2 * C == P and HID == P and CH == 2 and ADDS % 2 == 0 and UNITS % 4 == 0

    x_pairs = x.rearrange("(q two) c h w -> q (two c) (h w)", two=2)
    out_pairs = out.rearrange("(q two) c h w -> q (two c) (h w)", two=2)

    with ExitStack() as ctx:
        def sb(name, shape, dt):
            return ctx.enter_context(nc.sbuf_tensor(name, shape, dt))

        def bank(name, dt=F32, cols=CW):
            return ctx.enter_context(nc.psum_tensor(name, [P, cols], dt))

        def sem(name):
            return ctx.enter_context(nc.semaphore(name))

        ident = sb("ident", [P, P], F32)
        ident_b = sb("ident_b", [P, P], BF16)
        mean_col = sb("mean_col", [P, 2], F32)
        mean_mat = sb("mean_mat", [P, P], F32)
        center_mat = sb("center_mat", [P, P], F32)
        conv_raw = sb("conv_raw", [P, C * KH * KW], F32)
        conv_sign = sb("conv_sign", [P, len(TAPS), 2, C], BF16)
        conv_w = sb("conv_w", [P, 2, len(TAPS), P], BF16)
        bn_raw = sb("bn_raw", [P, 8], F32)
        bn = sb("bn", [P, 2, 2], F32)
        bn_tmp = sb("bn_tmp", [P, 2, 2], F32)
        gate_mat = sb("gate_mat", [P, 2, E], F32)
        gate_bias = sb("gate_bias", [P, E], F32)
        first_rank = sb("first_rank", [P, E], F32)
        rank_int = sb("rank_int", [P, E], mybir.dt.int32)
        up_raw = sb("up_raw", [P, 2, E, HID], F32)
        up_hi = sb("up_hi", [P, 2, E, HID], F32R)
        up_lo = sb("up_lo", [P, 2, E, HID], F32R)
        down_raw = sb("down_raw", [P, E, D], F32)
        down_hi = sb("down_hi", [P, E, D], F16)
        down_lo = sb("down_lo", [P, E, D], F16)
        largest = sb("largest", [P, 3], F32)
        largest_all = sb("largest_all", [P, 3], F32)
        scales = sb("scales", [P, 2], F32)
        unscale = sb("unscale", [P, 3], F32)
        warm = sb("warm", [P, 2], F32)
        start = sb("start", [P, 13], F32)

        x_in = sb("x_in", [P, HW], F32)
        xc = sb("xc", [P, HW], F32)
        sq = sb("sq", [P, HW], F32)
        var_eps = sb("var_eps", [P, 2, CH, TPC, 2], F32)
        rstd_wide = sb("rstd_wide", [P, CH, 2 * TPC, C], F32)
        ones = sb("ones", [P, 2], F32)
        minus_half = sb("minus_half", [P, 2 * TPC], F32)
        rstd = sb("rstd", [P, 2, CH, TPC, 2], F32)
        x_ln = sb("x_ln", [P, HW], F32)
        bn_sum = sb("bn_sum", [P, HW], F32)
        sign1 = sb("sign1", [P, H + 1, W + 2], BF16)
        sign2 = sb("sign2", [P, H + 1, W + 2], BF16)
        x2 = sb("x2", [P, HW], F32)
        x2_keep = sb("x2_keep", [P, HW], F32)
        xn = sb("xn", [P, HW], F32)
        xs = sb("xs", [P, GROUPS, CW], F32R)
        logits = sb("logits", [P, 2 * TILES, E], F32)
        match = sb("match", [P, 2 * TILES, E], F32)
        key = sb("key", [P, 2 * TILES, E], F32)
        pick1 = sb("pick1", [P, 2 * TILES, E], F32)
        pick2 = sb("pick2", [P, 2 * TILES, E], F32)
        top = sb("top", [P, 8, 2 * TILES], F32)
        disp = sb("disp", [P, TILES, 2, E], F32)

        act_s = [sb(f"act_s{i}", [P, CW], F32) for i in range(2)]
        hidden = [sb(f"hidden{i}", [P, CW], F32) for i in range(4)]
        hidden_hi = [sb(f"hidden_hi{i}", [P, CW], F16) for i in range(RING)]
        hidden_lo = [sb(f"hidden_lo{i}", [P, CW], F16) for i in range(RING)]
        weighted = [sb(f"weighted{i}", [P, TPC, 2, D], F32) for i in range(2)]
        acc = [sb(f"acc{i}", [P, TPC, 2, D], F32) for i in range(2)]
        ffn = sb("ffn", [P, TILES, 2, D], F32)
        out_sb = [sb(f"out_sb{i}", [P, CW], F32) for i in range(CH)]

        up1 = [bank(f"up1_{i}") for i in range(2)]
        up2 = [bank(f"up2_{i}") for i in range(2)]
        down = [bank(f"down_{i}") for i in range(2)]
        misc = [bank(f"misc_{i}") for i in range(2)]

        consts_in = sem("consts_in")
        conv_in = sem("conv_in")
        up_in = sem("up_in")
        x_loaded = sem("x_loaded")
        stored = [sem(f"stored{c}") for c in range(CH)]
        pool_made = sem("pool_made")
        dve_made = sem("dve_made")
        taps_signed = sem("taps_signed")
        taps_turned = sem("taps_turned")
        hi_made = sem("hi_made")
        weights_made = sem("weights_made")
        WM_LARGEST, WM_W2, WM_UP, WM_ALL = 4, 13, 15, 18
        reduced = sem("reduced")
        center_ready, center_read = sem("center_ready"), sem("center_read")
        var_ready, var_read = sem("var_ready"), sem("var_read")
        conv1_ready, conv1_read = sem("conv1_ready"), sem("conv1_read")
        conv2_ready, conv2_read = sem("conv2_ready"), sem("conv2_read")
        center2_ready, center2_read = sem("center2_ready"), sem("center2_read")
        var2_ready, var2_read = sem("var2_ready"), sem("var2_read")
        norm_ready, norm2_ready = sem("norm_ready"), sem("norm2_ready")
        gate_ready, gate_read = sem("gate_ready"), sem("gate_read")
        back_ready = [sem(f"back_ready{c}") for c in range(CH)]
        back_read = [sem(f"back_read{c}") for c in range(CH)]
        rstd_ready, rstd2_ready = sem("rstd_ready"), sem("rstd2_ready")
        powed = sem("powed")
        x_ln_ready = sem("x_ln_ready")
        relu_ready = sem("relu_ready")
        x2_ready = sem("x2_ready")
        x2_kept = sem("x2_kept")
        xn_ready = sem("xn_ready")
        xs_hi_ready = sem("xs_hi_ready")
        xs_ready = sem("xs_ready")
        gap_ready = sem("gap_ready")
        tanh_ready = sem("tanh_ready")
        disp_done = sem("disp_done")
        route_link = sem("route_link")
        up1_ready = sem("up1_ready")
        up2_ready = sem("up2_ready")
        silu_done = sem("silu_done")
        hidden_done = sem("hidden_done")
        hi_done = sem("hi_done")
        lo_done = [sem(f"lo_done{i}") for i in range(2)]
        down_done = sem("down_done")
        weighted_done = sem("weighted_done")
        added = sem("added")
        ffn_done = sem("ffn_done")

        block = ctx.enter_context(nc.Block())

        def turned(eng, front, slot, finish):
            front()
            for k in range(TURN):
                slot(k, 0, 0, False)
            if PAIRS > 1:
                with eng.Fori(0, PAIRS - 1) as p:
                    for k in range(TURN, SLOTS):
                        slot(k, p, p + 1, True)
                    for k in range(TURN):
                        slot(k, p + 1, p + 1, True)
            for k in range(TURN, SLOTS):
                slot(k, PAIRS - 1, 0, False)
            finish()

        def steps_of(engine, k, looped):
            if k < TURN:
                k += SLOTS
                if not looped:
                    return []
            steps = [(name, c) for at, here in PLAN.items() for name, c in here
                     if at + LATER[engine].get(name, 0) == k]
            return [s for s in steps if looped or s[0] in ("residual", "back")]

        def before(n, lag, total, p):
            if n >= lag:
                return n - lag, p
            return None if isinstance(p, int) else (n - lag + total, p - 1)

        def cols(c):
            return slice(c * CW, (c + 1) * CW)

        @block.sync
        def _(sp):
            sp.dma_start(x_in[:, :], x_pairs[0]).then_inc(x_loaded, 16)
            sp.dma_start(conv_raw[0:C, :], w1.rearrange("o c i j -> o (c i j)")).then_inc(conv_in, 16)
            sp.dma_start(conv_raw[C:P, :], w2.rearrange("o c i j -> o (c i j)")).then_inc(conv_in, 16)
            for m, w in enumerate((ffn_w1, ffn_w2)):
                for half in range(2):
                    sp.dma_start(up_raw[half * D:(half + 1) * D, m, :, :],
                                 w.rearrange("e d h -> d e h")).then_inc(up_in, 16)
            sp.dma_start(down_raw[:, :, :], ffn_w3.rearrange("e h d -> h e d")).then_inc(up_in, 16)

            def store(c, p):
                sp.wait_ge(back_read[c], p + 2)
                sp.dma_start(out_pairs[p, :, cols(c)], out_sb[c][:, :]).then_inc(stored[c], 16)

            def load(q):
                sp.wait_ge(x2_ready, CH * q)
                sp.dma_start(x_in[:, :], x_pairs[q]).then_inc(x_loaded, 16)

            load(1)
            with sp.Fori(0, PAIRS - 2) as p:
                load(p + 2)
                for c in range(CH):
                    store(c, p)
            for p in range(PAIRS - 2, PAIRS):
                for c in range(CH):
                    store(c, p)
            for c in range(CH):
                sp.wait_ge(stored[c], 16 * PAIRS + 16)

        @block.gpsimd
        def _(pool):
            for i, v in enumerate((gamma1, beta1, mean1, var1, gamma2, beta2, mean2, var2)):
                for half in range(2):
                    pool.dma_start(bn_raw[half * C:(half + 1) * C, i:i + 1],
                                   v.rearrange("(c one) -> c one", one=1)).then_inc(consts_in, 16)
            pool.memset(gate_mat[:, :, :], 0.0).then_inc(pool_made, 1)
            pool.memset(ident[:, :], 0.0).then_inc(pool_made, 1)
            pool.memset(mean_mat[:, :], 0.0).then_inc(pool_made, 1)
            pool.memset(mean_col[:, :], 0.0).then_inc(pool_made, 1)
            pool.memset(minus_half[:, :], -0.5).then_inc(pool_made, 1)
            pool.memset(ones[:, :], 1.0).then_inc(pool_made, 1)
            pool.memset(conv_w[:, :, :, :], 0.0).then_inc(pool_made, 1)
            pool.iota(rank_int[:, :], [[-1, E]], base=E, channel_multiplier=0).then_inc(pool_made, 1)
            pool.wait_ge(pool_made, 8)
            for half in range(2):
                pool.wait_ge(pool_made, 8 + 2 * half)
                pool.dma_start(gate_mat[half * D:(half + 1) * D, half, :], gate_w).then_inc(consts_in, 16)
                pool.memset(mean_mat[half * C:(half + 1) * C, half * C:(half + 1) * C], 1.0 / C)\
                    .then_inc(pool_made, 1)
                pool.memset(mean_col[half * C:(half + 1) * C, half:half + 1], 1.0 / C).then_inc(pool_made, 1)
            pool.dma_start(gate_bias[:, :], gate_b.partition_broadcast(P)).then_inc(consts_in, 16)
            pool.wait_ge(pool_made, 12)
            pool.affine_select(out=ident[:, :], in_=ident[:, :], compare_op=ALU.not_equal, fill=1.0,
                               base=0, pattern=[[-1, P]], channel_multiplier=1).then_inc(pool_made, 1)
            pool.wait_ge(consts_in, 16 * 19)
            pool.wait_ge(pool_made, 13)
            pool.wait_ge(dve_made, 7)
            pool.tensor_tensor(bn_tmp[:, :, 0:1], bn_tmp[:, :, 0:1],
                               minus_half[:, 0:2].unsqueeze(2), ALU.pow).then_inc(pool_made, 1)

            def step(name, c, p, q):
                if name in ("var", "var2"):
                    n = 0 if name == "var" else 1
                    pool.wait_ge((var_read, var2_read)[n], CH * q + c + 1)
                    pool.tensor_tensor(rstd[:, n, c, :, :], var_eps[:, n, c, :, :],
                                       minus_half[:, :].rearrange("p (t a) -> p t a", a=2), ALU.pow).then_inc(powed, 1)
                elif name == "conv2":
                    pool.wait_ge(x2_kept, CH * q)
                    pool.wait_ge(relu_ready, CH * q + c + 1)
                    pool.tensor_tensor(x2[:, cols(c)], x_in[:, cols(c)], bn_sum[:, cols(c)], ALU.add)\
                        .then_inc(x2_ready, 1)

            def front():
                for name in STAGE_STEPS:
                    for c in range(CH):
                        step(name, c, 0, 0)
                    if name == "var":
                        pool.wait_ge(weights_made, WM_LARGEST)
                        pool.partition_all_reduce(largest_all[:, :], largest[:, :], P, bass.bass_isa.ReduceOp.max)\
                            .then_inc(reduced, 1)

            def low_part(u, p):
                pool.wait_ge(hi_done, UNITS * p + u + 1)
                pool.tensor_tensor(hidden_lo[u % RING][:, :], hidden[u % 4][:, :], hidden_hi[u % RING][:, :],
                                   ALU.subtract).then_inc(lo_done[0], 1)

            def add_up(k, p):
                group, ep = k // EP, k % EP
                if ep > 0:
                    n = (EP - 1) * group + ep - 1
                    pool.wait_ge(weighted_done, SLOTS * p + k + 3)
                    if ep > 1:
                        pool.wait_ge(added, ADDS * p + n + 2)
                    pool.tensor_tensor(acc[group % 2][:, :, :, :], acc[group % 2][:, :, :, :],
                                       weighted[n % 2][:, :, :, :], ALU.add).then_inc(added, 1)
                if ep == EP - 1:
                    chunk, image = group // 2, group % 2
                    pool.wait_ge(back_ready[chunk], p + 1)
                    pool.wait_ge(added, ADDS * p + (EP - 1) * (group + 1) + 2)
                    pool.tensor_tensor(ffn[:, chunk * TPC:(chunk + 1) * TPC, image, :],
                                       acc[group % 2][:, :, 0, :], acc[group % 2][:, :, 1, :], ALU.add)\
                        .then_inc(ffn_done, 1)

            def slot(k, p, q, looped):
                if at := before(2 * k, LO_LAG, UNITS, p):
                    low_part(*at)
                if at := before(k, WEIGH_LAG, SLOTS, p):
                    add_up(*at)
                for name, c in steps_of("Pool", k, looped):
                    step(name, c, p - 1 if (name, c) == ("back", 1) else p, q)

            def finish():
                low_part(UNITS - 2, PAIRS - 1)
                for k in range(SLOTS - WEIGH_LAG, SLOTS):
                    add_up(k, PAIRS - 1)

            turned(pool, front, slot, finish)

        @block.scalar
        def _(act):
            act.wait_ge(dve_made, 1)
            act.activation(warm[:, 1:2], warm[:, 0:1], ACT.Silu).then_inc(silu_done, 2)
            act.wait_ge(dve_made, 11)
            act.wait_ge(conv_in, 32)
            for half in range(2):
                act.activation(conv_sign[:, :, half, :],
                               conv_raw[:, :].rearrange("p (c t) -> p t c", t=len(TAPS)), ACT.Sign)\
                    .then_inc(taps_signed, 1)

            def make_hi():
                act.wait_ge(weights_made, WM_W2)
                for m in range(2):
                    act.activation(up_hi[:, m, :, :], up_raw[:, m, :, :], ACT.Copy).then_inc(hi_made, 1)
                act.activation(down_hi[:, :, :], down_raw[:, :, :], ACT.Copy).then_inc(hi_made, 1)

            def step(name, c, p, q):
                if name == "residual":
                    act.wait_ge(back_read[c], p + 1)
                    act.wait_ge(x2_ready, CH * (p + 1))
                    act.activation(x2_keep[:, cols(c)], x2[:, cols(c)], ACT.Copy).then_inc(x2_kept, 1)
                elif name in ("var", "var2"):
                    n = 0 if name == "var" else 1
                    act.wait_ge(powed, 2 * CH * q + CH * n + c + 1)
                    act.activation(rstd_wide[:, c, :, :],
                                   rstd[:, n, c, :, :].rearrange("p t a -> p (t a)").unsqueeze(2)
                                   .to_broadcast([P, 2 * TPC, C]), ACT.Copy)\
                        .then_inc((rstd_ready, rstd2_ready)[n], 1)
                elif name == "center":
                    act.wait_ge(center_ready, CH * q + c + 1)
                    act.wait_ge(xn_ready, CH * q)
                    act.activation(sq[:, cols(c)], misc[c][:, :], ACT.Square)
                    act.activation(sign1[:, c * ROWS:(c + 1) * ROWS, 1:W + 1],
                                   misc[c][:, :].rearrange("p (h w) -> p h w", w=W), ACT.Sign)
                    act.activation(xc[:, cols(c)], misc[c][:, :], ACT.Copy).then_inc(center_read, 1)
                elif name == "conv2":
                    act.wait_ge(conv2_read, CH * q + c + 1)
                    act.activation(bn_sum[:, cols(c)], bn_sum[:, cols(c)], ACT.Relu, bias=bn[:, 1, 1:2])\
                        .then_inc(relu_ready, 1)
                elif name == "center2":
                    act.wait_ge(center2_ready, CH * q + c + 1)
                    act.activation(sq[:, cols(c)], misc[c][:, :], ACT.Square)
                    act.activation(xc[:, cols(c)], misc[c][:, :], ACT.Copy).then_inc(center2_read, 1)
                elif name == "split":
                    chunk, image = c // 2, c % 2
                    rows = slice(image * D, (image + 1) * D)
                    act.wait_ge(xn_ready, CH * (q + 1))
                    if not isinstance(q, int) or q > 0:
                        act.wait_ge(up2_ready, UNITS * q - UNITS + 2 * EP * (c + 1))
                    act.activation(xs[rows, c, :], xn[rows, cols(chunk)], ACT.Copy).then_inc(xs_hi_ready, 1)
                elif name == "route" and c == 6:
                    act.wait_ge(gap_ready, q + 1)
                    act.activation(top[:, 5, :], top[:, 4, :], ACT.Tanh, scale=0.5).then_inc(tanh_ready, 1)

            def front():
                for name in STAGE_STEPS:
                    for c in range({"split": GROUPS, "route": ROUTE_PARTS}.get(name, CH)):
                        step(name, c, 0, 0)
                    if name == "conv1":
                        make_hi()

            def high_part(u, p):
                act.wait_ge(hidden_done, UNITS * p + u + 3)
                act.wait_ge(down_done, UNITS * p + u + 1)
                act.activation(hidden_hi[u % RING][:, :], hidden[u % 4][:, :], ACT.Copy).then_inc(hi_done, 1)

            def slot(k, p, q, looped):
                for u in (2 * k, 2 * k + 1):
                    act.wait_ge(up1_ready, UNITS * p + u + 1)
                    act.wait_ge(hidden_done, UNITS * p + u + 1)
                    act.activation(act_s[u % 2][:, :], up1[u % 2][:, :], ACT.Silu).then_inc(silu_done, 1)
                    if at := before(u, HI_LAG, UNITS, p):
                        high_part(*at)
                for name, c in steps_of("ScalarE", k, looped):
                    step(name, c, p - 1 if (name, c) == ("back", 1) else p, q)

            turned(act, front, slot, lambda: high_part(UNITS - 1, PAIRS - 1))

        @block.tensor
        def _(pe):
            pe.wait_ge(pool_made, 13)
            pe.wait_ge(dve_made, 6)

            def transpose_taps():
                pe.wait_ge(taps_signed, 2)
                turned_taps = misc[1][:, :].bitcast(BF16)
                for t in range(len(TAPS)):
                    last = pe.transpose(turned_taps[:, t * P:(t + 1) * P],
                                        conv_sign[:, t, :, :].rearrange("p a c -> p (a c)"), ident_b[:, :])
                last.then_inc(taps_turned, 1)

            def conv(c, which, image):
                for t, (i, j) in enumerate(TAPS):
                    last = pe.matmul(misc[c][:, :], conv_w[:, which, t, :],
                                     image[:, c * ROWS + i:(c + 1) * ROWS + i, j:j + W],
                                     start=(t == 0), stop=(t == len(TAPS) - 1))
                return last

            def step(name, c, p, q):
                if name == "center":
                    pe.wait_ge(x_loaded, 16 * (q + 1))
                    pe.wait_ge(gate_read, q)
                    if not isinstance(q, int):
                        pe.wait_ge(back_read[c], p + 1)
                    pe.matmul(misc[c][:, :], center_mat[:, :], x_in[:, cols(c)], start=True, stop=True)\
                        .then_inc(center_ready, 1)
                elif name in ("var", "var2"):
                    n = 0 if name == "var" else 1
                    pe.wait_ge((center_read, center2_read)[n], CH * q + c + 1)
                    for t in range(TPC):
                        last = pe.matmul(misc[c][:, 2 * t:2 * t + 2],
                                         sq[:, c * CW + t * P:c * CW + (t + 1) * P], mean_col[:, :],
                                         start=True, stop=True)
                    last.then_inc((var_ready, var2_ready)[n], 1)
                elif name in ("norm", "norm2"):
                    n = 0 if name == "norm" else 1
                    pe.wait_ge((conv1_read, var2_read)[n], CH * q + c + 1)
                    pe.wait_ge((rstd_ready, rstd2_ready)[n], CH * q + c + 1)
                    for t in range(TPC):
                        last = pe.transpose(misc[c][:, t * P:(t + 1) * P],
                                            rstd_wide[:, c, 2 * t:2 * t + 2, :].rearrange("p a c -> p (a c)"),
                                            ident[:, :])
                    last.then_inc((norm_ready, norm2_ready)[n], 1)
                elif name == "conv1":
                    pe.wait_ge(var_read, CH * q + c + 1)
                    pe.wait_ge(center_read, CH * (q + 1))
                    conv(c, 0, sign1).then_inc(conv1_ready, 1)
                elif name == "conv2":
                    pe.wait_ge(conv1_read, CH * (q + 1))
                    pe.wait_ge(x_ln_ready, CH * q + c + 1)
                    conv(c, 1, sign2).then_inc(conv2_ready, 1)
                elif name == "center2":
                    pe.wait_ge(conv2_read, CH * q + c + 1)
                    pe.wait_ge(x2_ready, CH * q + c + 1)
                    pe.matmul(misc[c][:, :], center_mat[:, :], x2[:, cols(c)], start=True, stop=True)\
                        .then_inc(center2_ready, 1)
                elif name == "gate" and c == 0:
                    pe.wait_ge(xn_ready, CH * (q + 1))
                    for j in range(TILES):
                        last = pe.matmul(misc[0][:, j * 2 * E:(j + 1) * 2 * E], xn[:, j * P:(j + 1) * P],
                                         gate_mat[:, :, :].rearrange("p a e -> p (a e)"), start=True, stop=True)
                    last.then_inc(gate_ready, 1)
                elif name == "back":
                    pe.wait_ge(ffn_done, GROUPS * p + 2 * (c + 1) + 2)
                    if c == 0:
                        pe.wait_ge(gate_read, q + 1 if not isinstance(q, int) else PAIRS)
                    else:
                        pe.wait_ge(xn_ready, CH * (q + 1) if not isinstance(q, int) else CH * PAIRS)
                    for t in range(TPC):
                        last = pe.transpose(misc[c][:, t * P:(t + 1) * P],
                                            ffn[:, c * TPC + t, :, :].rearrange("p a d -> p (a d)"), ident[:, :])
                    last.then_inc(back_ready[c], 1)

            def front():
                for name in STAGE_STEPS:
                    for c in range(CH):
                        step(name, c, 0, 0)
                    if name == "center":
                        pe.wait_ge(center_read, CH)
                        transpose_taps()
                        pe.wait_ge(weights_made, 1)

            def down_product(u, p):
                k, e = u // 2, u % E
                pe.wait_ge(lo_done[u % 2], UNITS // 2 * p + u // 2 + 3)
                if u % 2 == 0:
                    pe.wait_ge(weighted_done, SLOTS * p + k + 1)
                parts = ((hidden_hi, down_hi), (hidden_hi, down_lo), (hidden_lo, down_hi))
                for t in range(TPC):
                    for n, (h, w) in enumerate(parts):
                        last = pe.matmul(down[k % 2][:, (2 * t + u % 2) * D:(2 * t + u % 2 + 1) * D],
                                         h[u % RING][:, t * P:(t + 1) * P], w[:, e, :],
                                         start=(n == 0), stop=(n == len(parts) - 1))
                last.then_inc(down_done, 1)

            def slot(k, p, q, looped):
                group = k // EP
                if k == 0 and isinstance(p, int):
                    pe.wait_ge(weights_made, WM_ALL)
                if k % EP == 0:
                    pe.wait_ge(xs_ready, GROUPS * p + group + 1)
                for u in (2 * k, 2 * k + 1):
                    e = u % E
                    for m, (banks, free, ready) in enumerate(((up1, silu_done, up1_ready),
                                                              (up2, hidden_done, up2_ready))):
                        pe.wait_ge(free, UNITS * p + u + 1)
                        pe.matmul(banks[u % 2][:, :], up_hi[:, m, e, :], xs[:, group, :], start=True, stop=False)
                        pe.matmul(banks[u % 2][:, :], up_lo[:, m, e, :], xs[:, group, :], start=False, stop=True)\
                            .then_inc(ready, 1)
                    if at := before(u, DOWN_LAG, UNITS, p):
                        down_product(*at)
                for name, c in steps_of("TensorE", k, looped):
                    step(name, c, p - 1 if (name, c) == ("back", 1) else p, q)

            def finish():
                for u in range(UNITS - DOWN_LAG, UNITS):
                    down_product(u, PAIRS - 1)
                step("back", 1, PAIRS - 1, 0)

            turned(pe, front, slot, finish)

        @block.vector
        def _(dve):
            dve.memset(warm[:, :], 0.0).then_inc(dve_made, 1)
            dve.memset(sign1[:, :, :], 0.0).then_inc(dve_made, 1)
            dve.memset(sign2[:, :, :], 0.0).then_inc(dve_made, 1)
            for i, (free, count) in enumerate(((hidden_done, 2), (down_done, RING), (added, 2),
                                               (lo_done[0], 2), (lo_done[1], 2),
                                               (weighted_done, 2), (ffn_done, 2),
                                               (back_ready[0], 1), (back_ready[1], 1), (back_read[0], 1),
                                               (back_read[1], 1), (stored[0], 16), (stored[1], 16))):
                dve.memset(start[:, i:i + 1], 0.0).then_inc(free, count)
            dve.wait_ge(pool_made, 13)
            dve.tensor_copy(ident_b[:, :], ident[:, :]).then_inc(dve_made, 1)
            dve.tensor_tensor(center_mat[:, :], ident[:, :], mean_mat[:, :], ALU.subtract).then_inc(dve_made, 1)
            dve.tensor_copy(first_rank[:, :], rank_int[:, :]).then_inc(dve_made, 1)
            dve.wait_ge(consts_in, 16 * 19)
            raw = bn_raw[:, :].rearrange("p (k v) -> p k v", k=2)
            dve.tensor_scalar(bn_tmp[:, :, 0:1], raw[:, :, 3:4], EPS_BN, None, ALU.add).then_inc(dve_made, 1)
            dve.wait_ge(pool_made, 14)
            dve.tensor_tensor(bn[:, :, 0:1], bn_tmp[:, :, 0:1], raw[:, :, 0:1], ALU.mult).then_inc(dve_made, 1)
            dve.wait_ge(dve_made, 8)
            dve.tensor_tensor(bn_tmp[:, :, 1:2], raw[:, :, 2:3], bn[:, :, 0:1], ALU.mult).then_inc(dve_made, 1)
            dve.wait_ge(dve_made, 9)
            dve.tensor_tensor(bn[:, 0, 1:2], bn_tmp[:, 0, 1:2], raw[:, 0, 1:2], ALU.subtract).then_inc(dve_made, 1)
            dve.tensor_tensor(bn[:, 1, 1:2], raw[:, 1, 1:2], bn_tmp[:, 1, 1:2], ALU.subtract).then_inc(dve_made, 1)
            dve.wait_ge(dve_made, 11)

            def place_taps():
                dve.wait_ge(taps_turned, 1)
                turned_taps = misc[1][:, :].bitcast(BF16)[:, 0:len(TAPS) * P]
                turned_taps = turned_taps.rearrange("p (t k o) -> p t k o", t=len(TAPS), k=2)
                for half in range(2):
                    rows = slice(half * C, (half + 1) * C)
                    for k in range(2):
                        last = dve.tensor_copy(conv_w[rows, k, :, rows], turned_taps[rows, :, k, :])
                last.then_inc(weights_made, 1)

            def find_scales():
                dve.wait_ge(up_in, 16 * 5)
                for m in range(2):
                    dve.tensor_reduce(largest[:, m:m + 1], up_raw[:, m, :, :].rearrange("p e h -> p (e h)"),
                                      AX.X, ALU.max, apply_absolute_value=True).then_inc(weights_made, 1)
                dve.tensor_reduce(largest[:, 2:3], down_raw[:, :, :].rearrange("p e d -> p (e d)"),
                                  AX.X, ALU.max, apply_absolute_value=True).then_inc(weights_made, 1)
                dve.wait_ge(reduced, 1)

            def scale_weights():
                def then(ins, count):
                    ins.then_inc(weights_made, 1)
                    dve.wait_ge(weights_made, count)
                then(dve.tensor_scalar(largest[:, :], largest_all[:, :], LEAST_WEIGHT, None, ALU.max), 5)
                then(dve.tensor_tensor(largest[:, 1:2], largest[:, 0:1], largest[:, 1:2], ALU.mult), 6)
                then(dve.reciprocal(scales[:, :], largest[:, 1:3]), 7)
                then(dve.tensor_scalar(scales[:, 0:1], scales[:, 0:1], 2.0 ** 15 / D ** 2, None, ALU.mult), 8)
                then(dve.tensor_scalar(scales[:, 1:2], scales[:, 1:2], 2.0 ** 14, None, ALU.mult), 9)
                then(dve.tensor_scalar(scales[:, :].bitcast(U32), scales[:, :].bitcast(U32), EXPONENT_BITS, None,
                                       ALU.bitwise_and), 10)
                then(dve.tensor_tensor(unscale[:, 0:1], scales[:, 0:1], scales[:, 1:2], ALU.mult), 11)
                dve.tensor_scalar(down_raw[:, :, :], down_raw[:, :, :], scales[:, 1:2], None, ALU.mult)\
                    .then_inc(weights_made, 1)
                dve.tensor_scalar(up_raw[:, 1, :, :], up_raw[:, 1, :, :], scales[:, 0:1], None, ALU.mult)\
                    .then_inc(weights_made, 1)

            def make_lo():
                for m in range(2):
                    dve.wait_ge(hi_made, m + 1)
                    dve.tensor_tensor(up_lo[:, m, :, :], up_raw[:, m, :, :], up_hi[:, m, :, :].bitcast(F32),
                                      ALU.subtract).then_inc(weights_made, 1)
                dve.wait_ge(hi_made, 3)
                dve.tensor_tensor(down_lo[:, :, :], down_raw[:, :, :], down_hi[:, :, :], ALU.subtract)\
                    .then_inc(weights_made, 1)
                dve.reciprocal(unscale[:, 1:2], unscale[:, 0:1]).then_inc(weights_made, 1)
                dve.wait_ge(weights_made, WM_ALL - 1)
                dve.tensor_scalar(unscale[:, 2:3], unscale[:, 1:2], -0.5, None, ALU.mult).then_inc(weights_made, 1)
                dve.wait_ge(weights_made, WM_ALL)
                dve.tensor_scalar(unscale[:, 1:2], unscale[:, 1:2], 0.5, None, ALU.mult).then_inc(weights_made, 1)
                dve.wait_ge(weights_made, WM_ALL + 1)

            LINKS = 15

            def spread(a):
                return a.unsqueeze(2).to_broadcast([P, 2 * TILES, E])

            def ranks():
                return first_rank[:, :].unsqueeze(1).to_broadcast([P, 2 * TILES, E])

            def pick_first(n, best, pick, q, at):
                if n == 0:
                    dve.tensor_reduce(best, logits[:, :, :], AX.X, ALU.max).then_inc(route_link, 1)
                    dve.wait_ge(route_link, LINKS * q + at)
                    dve.tensor_tensor(match[:, :, :], logits[:, :, :], spread(best), ALU.is_equal)\
                        .then_inc(route_link, 1)
                elif n == 1:
                    dve.wait_ge(route_link, LINKS * q + at + 1)
                    dve.tensor_tensor(key[:, :, :], match[:, :, :], ranks(), ALU.mult).then_inc(route_link, 1)
                    dve.wait_ge(route_link, LINKS * q + at + 2)
                    dve.tensor_reduce(top[:, 7, :], key[:, :, :], AX.X, ALU.max).then_inc(route_link, 1)
                else:
                    dve.wait_ge(route_link, LINKS * q + at + 3)
                    dve.tensor_tensor(pick[:, :, :], key[:, :, :], spread(top[:, 7, :]), ALU.is_equal)\
                        .then_inc(route_link, 1)

            def step(name, c, p, q):
                if name in ("var", "var2"):
                    n = 0 if name == "var" else 1
                    dve.wait_ge((var_ready, var2_ready)[n], CH * q + c + 1)
                    dve.tensor_scalar(var_eps[:, n, c, :, :],
                                      misc[c][:, 0:2 * TPC].rearrange("p (t a) -> p t a", a=2),
                                      (EPS_CONV_LN, EPS_TOKEN_LN)[n], None, ALU.add)\
                        .then_inc((var_read, var2_read)[n], 1)
                elif name == "norm":
                    dve.wait_ge(norm_ready, CH * q + c + 1)
                    dve.tensor_tensor(x_ln[:, cols(c)], misc[c][:, :], xc[:, cols(c)], ALU.mult)\
                        .then_inc(x_ln_ready, 1)
                elif name == "norm2":
                    dve.wait_ge(norm2_ready, CH * q + c + 1)
                    dve.tensor_tensor(xn[:, cols(c)], misc[c][:, :], xc[:, cols(c)], ALU.mult)\
                        .then_inc(xn_ready, 1)
                elif name == "conv1":
                    dve.wait_ge(conv1_ready, CH * q + c + 1)
                    dve.tensor_scalar(sign2[:, c * ROWS:(c + 1) * ROWS, 1:W + 1],
                                      misc[c][:, :].rearrange("p (h w) -> p h w", w=W),
                                      bn[:, 0, 0:1], bn[:, 0, 1:2], ALU.mult, ALU.is_gt).then_inc(conv1_read, 1)
                elif name == "conv2":
                    dve.wait_ge(conv2_ready, CH * q + c + 1)
                    dve.wait_ge(x_ln_ready, CH * q + c + 1)
                    dve.scalar_tensor_tensor(out=bn_sum[:, cols(c)], in0=misc[c][:, :], scalar=bn[:, 1, 0:1],
                                             in1=x_ln[:, cols(c)], op0=ALU.mult, op1=ALU.add)\
                        .then_inc(conv2_read, 1)
                elif name == "gate" and c == 0:
                    dve.wait_ge(gate_ready, q + 1)
                    dve.tensor_tensor(logits[:, :, :],
                                      misc[0][:, 0:2 * TILES * E].rearrange("p (t e) -> p t e", e=E),
                                      gate_bias[:, :].unsqueeze(1).to_broadcast([P, 2 * TILES, E]), ALU.add)\
                        .then_inc(gate_read, 1)
                elif name == "split":
                    chunk, image = c // 2, c % 2
                    rows = slice(image * D, (image + 1) * D)
                    other = slice((1 - image) * D, (2 - image) * D)
                    dve.wait_ge(xs_hi_ready, GROUPS * q + c + 1)
                    dve.tensor_tensor(xs[other, c, :], xn[rows, cols(chunk)], xs[rows, c, :].bitcast(F32),
                                      ALU.subtract).then_inc(xs_ready, 1)
                elif name == "route" and c < 3:
                    if c == 0:
                        dve.wait_ge(gate_read, q + 1)
                    pick_first(c, top[:, 0, :], pick1, q, 1)
                    if c == 2:
                        dve.wait_ge(route_link, LINKS * q + 5)
                        dve.scalar_tensor_tensor(out=logits[:, :, :], in0=pick1[:, :, :], scalar=MASKED,
                                                 in1=logits[:, :, :], op0=ALU.mult, op1=ALU.add)\
                            .then_inc(route_link, 1)
                elif name == "route" and c < 6:
                    dve.wait_ge(route_link, LINKS * q + 6)
                    pick_first(c - 3, top[:, 1, :], pick2, q, 7)
                    if c == 3:
                        dve.tensor_tensor(top[:, 4, :], top[:, 0, :], top[:, 1, :], ALU.subtract)\
                            .then_inc(gap_ready, 1)
                elif name == "route" and c == 6:
                    dve.wait_ge(tanh_ready, q + 1)
                    dve.tensor_scalar(top[:, 2, :], top[:, 5, :], unscale[:, 1:2], unscale[:, 1:2],
                                      ALU.mult, ALU.add).then_inc(route_link, 1)
                    dve.tensor_scalar(top[:, 3, :], top[:, 5, :], unscale[:, 2:3], unscale[:, 1:2],
                                      ALU.mult, ALU.add).then_inc(route_link, 1)
                elif name == "route" and c == 7:
                    dve.wait_ge(route_link, LINKS * q + 13)
                    dve.tensor_tensor(pick1[:, :, :], pick1[:, :, :], spread(top[:, 2, :]), ALU.mult)\
                        .then_inc(route_link, 1)
                    dve.tensor_tensor(pick2[:, :, :], pick2[:, :, :], spread(top[:, 3, :]), ALU.mult)\
                        .then_inc(route_link, 1)
                elif name == "dispatch":
                    dve.wait_ge(route_link, LINKS * q + LINKS)
                    dve.wait_ge(weighted_done, SLOTS * q + 2)
                    dve.tensor_tensor(disp[:, :, :, :].rearrange("p t a e -> p (t a) e"), pick1[:, :, :],
                                      pick2[:, :, :], ALU.add).then_inc(disp_done, 1)
                elif name == "back":
                    dve.wait_ge(back_ready[c], p + 2)
                    dve.wait_ge(x2_kept, CH * p + c + 1)
                    dve.wait_ge(stored[c], 16 * p + 16)
                    dve.tensor_tensor(out_sb[c][:, :], misc[c][:, :], x2_keep[:, cols(c)], ALU.add)\
                        .then_inc(back_read[c], 1)

            def front():
                for name in STAGE_STEPS:
                    for c in range({"split": GROUPS, "route": ROUTE_PARTS}.get(name, CH)):
                        step(name, c, 0, 0)
                    if name == "center":
                        place_taps()
                    if name == "var":
                        find_scales()
                    if name == "conv1":
                        scale_weights()
                    if name == "norm":
                        make_lo()
                step("dispatch", 0, 0, 0)

            def weigh(k, p):
                group, ep = k // EP, k % EP
                chunk, image = group // 2, group % 2
                dve.wait_ge(down_done, UNITS * p + 2 * k + 2 + RING)
                weights = disp[:, chunk * TPC:(chunk + 1) * TPC, image, 2 * ep:2 * ep + 2]
                weights = weights.unsqueeze(3).to_broadcast([P, TPC, 2, D])
                if k == 0:
                    dve.wait_ge(disp_done, p + 1)
                if ep == 0:
                    dve.wait_ge(ffn_done, GROUPS * p + group + 1)
                    dst = acc[group % 2]
                else:
                    n = (EP - 1) * group + ep - 1
                    dve.wait_ge(added, ADDS * p + n + 1)
                    dst = weighted[n % 2]
                dve.tensor_tensor(dst[:, :, :, :], down[k % 2][:, :].rearrange("p (t a d) -> p t a d", a=2, d=D),
                                  weights, ALU.mult).then_inc(weighted_done, 1)

            def low_part(u, p):
                dve.wait_ge(hi_done, UNITS * p + u + 1)
                dve.tensor_tensor(hidden_lo[u % RING][:, :], hidden[u % 4][:, :], hidden_hi[u % RING][:, :],
                                  ALU.subtract).then_inc(lo_done[1], 1)

            def slot(k, p, q, looped):
                if k == WEIGH_LAG and looped:
                    step("dispatch", 0, p, p)
                if at := before(k, WEIGH_LAG, SLOTS, p):
                    weigh(*at)
                for u in (2 * k, 2 * k + 1):
                    dve.wait_ge(silu_done, UNITS * p + u + 3)
                    dve.wait_ge(up2_ready, UNITS * p + u + 1)
                    dve.wait_ge(lo_done[u % 2], UNITS // 2 * p + u // 2 + 1)
                    dve.tensor_tensor(hidden[u % 4][:, :], act_s[u % 2][:, :], up2[u % 2][:, :], ALU.mult)\
                        .then_inc(hidden_done, 1)
                    if u % 2 == 1:
                        if at := before(u, LO_LAG, UNITS, p):
                            low_part(*at)
                for name, c in steps_of("VectorE", k, looped):
                    step(name, c, p - 1 if (name, c) == ("back", 1) else p, q)

            def finish():
                low_part(UNITS - 1, PAIRS - 1)
                for k in range(SLOTS - WEIGH_LAG, SLOTS):
                    weigh(k, PAIRS - 1)
                step("back", 1, PAIRS - 1, 0)

            turned(dve, front, slot, finish)


_INS = ["x", "L0_conv_w1", "L0_conv_gamma1", "L0_conv_beta1", "L0_conv_mean1", "L0_conv_var1",
        "L0_conv_w2", "L0_conv_gamma2", "L0_conv_beta2", "L0_conv_mean2", "L0_conv_var2",
        "L0_ffn_gate_w", "L0_ffn_gate_b", "L0_ffn_w1", "L0_ffn_w2", "L0_ffn_w3"]


def kernel(**inputs):
    import numpy as _np
    import concourse.bacc as _bacc
    from concourse import mybir as _mybir
    from concourse.bass_utils import run_bass_kernel_spmd as _run

    nc = _bacc.Bacc("TRN2", target_bir_lowering=False, num_devices=1)
    arrays, args = {}, []
    for name in _INS:
        a = _np.ascontiguousarray(inputs[name])
        arrays[f"in_{name}"] = a
        args.append(nc.dram_tensor(f"in_{name}", a.shape, _mybir.dt.from_np(a.dtype), kind="ExternalInput").ap())
    shape = arrays["in_x"].shape
    args.append(nc.dram_tensor("out_0", shape, _mybir.dt.float32, kind="ExternalOutput").ap())
    metaformer_kernel(nc, *args)
    r = _run(nc, [arrays], core_ids=[0])
    return r.results[0]["out_0"]
```

```python
from contextlib import ExitStack

import concourse.bass as bass
from concourse import mybir

ALU = mybir.AluOpType
ACT = mybir.ActivationFunctionType
AX = mybir.AxisListType
F32 = mybir.dt.float32
F32R = mybir.dt.float32r
BF16 = mybir.dt.bfloat16
F16 = mybir.dt.float16
U32 = mybir.dt.uint32

P = 128
EPS_CONV_LN = 1e-6
EPS_TOKEN_LN = 1e-5
EPS_BN = 1e-5
MASKED = -3.0e38
LEAST_WEIGHT = 2.0 ** -30
EXPONENT_BITS = 0x7F800000

PLAN = {
    "TensorE": {
        5: [("center", 0)], 6: [("center", 1)], 7: [("center", 2)], 8: [("var", 0), ("center", 3)],
        9: [("conv1", 0)], 10: [("var", 1)], 11: [("conv1", 1)], 12: [("conv1", 2)], 13: [("conv1", 3)],
        14: [("norm", 0)], 15: [("conv2", 0)], 16: [("conv2", 1)], 17: [("norm", 1)], 18: [("conv2", 2)],
        19: [("center2", 0), ("center2", 1)], 20: [("conv2", 3)], 21: [("var2", 0)], 22: [("back", 0)],
        23: [("norm2", 0), ("center2", 2)], 24: [("gate", 0)], 25: [("center2", 3)],
        27: [("var2", 1)], 29: [("norm2", 1)], 30: [("gate", 1)], 36: [("back", 1)],
    },
    "VectorE": {
        14: [("norm", 0)], 16: [("conv2", 0)], 17: [("norm", 1)], 20: [("conv2", 1)], 22: [("back", 0)],
        23: [("norm2", 0)], 24: [("split", 0), ("gate", 0)], 25: [("route", 0)],
        26: [("route", 1)], 27: [("route", 2)], 28: [("route", 3)], 29: [("norm2", 1)],
        30: [("gate", 1), ("route", 4)], 31: [("route", 5)],
        32: [("route", 6)], 33: [("route", 7)], 36: [("back", 1)], 37: [("split", 1)],
        38: [("route", 8)], 39: [("route", 9)], 40: [("route", 10)], 41: [("route", 11)],
        42: [("route", 12)], 43: [("route", 13)], 45: [("route", 14)], 47: [("route", 15)],
    },
    "ScalarE": {
        5: [("residual", 0)], 6: [("square", 0), ("sign", 0)], 7: [("copy", 0), ("residual", 1)],
        8: [("var", 0), ("square", 1), ("sign", 1)], 9: [("copy", 1), ("wide", 0)], 10: [("var", 1)],
        11: [("conv1", 0)], 12: [("wide", 1)], 13: [("conv1", 1)], 17: [("relu", 0)],
        20: [("square2", 0), ("copy2", 0)], 21: [("var2", 0), ("relu", 1)], 22: [("wide2", 0)],
        24: [("split", 0)], 25: [("square2", 1)], 26: [("copy2", 1)], 27: [("var2", 1)], 28: [("wide2", 1)],
        30: [("tanh", 0)], 36: [("split", 1)], 43: [("tanh", 1)],
    },
    "Pool": {
        8: [("var", 0)], 10: [("var", 1)], 17: [("x2", 0)], 21: [("var2", 0), ("x2", 1)], 27: [("var2", 1)],
    },
}
CATCH_UP = ((26, 27), (27, 29), (29, 35), (35, 36), (36, 37))
TURN = len(CATCH_UP)
ROUTE_PARTS = 8
HI_LAG = 1
LO_LAG = 2
DOWN_LAG = 4
WEIGH_LAG = 3
RING = 8


def metaformer_kernel(nc, x, w1, gamma1, beta1, mean1, var1, w2, gamma2, beta2, mean2, var2,
                      gate_w, gate_b, ffn_w1, ffn_w2, ffn_w3, out):
    B, C, H, W = x.shape
    E, D, HID = ffn_w1.shape
    _, _, KH, KW = w1.shape
    HW = H * W
    PAIRS = B // 2
    CW = 512
    CH = HW // CW
    ROWS = CW // W
    TPC = CW // P
    TILES = CH * TPC
    GROUPS = 2 * CH
    EP = E // 2
    SLOTS = GROUPS * EP
    UNITS = 2 * SLOTS
    ADDS = GROUPS * (EP - 1)
    TAPS = [(i, j) for i in range(KH) for j in range(KW)]
    assert C == D and 2 * C == P and HID == P and CH == 2 and ADDS % 2 == 0 and UNITS % 4 == 0

    x_pairs = x.rearrange("(q two) c h w -> q (two c) (h w)", two=2)
    out_pairs = out.rearrange("(q two) c h w -> q (two c) (h w)", two=2)

    with ExitStack() as ctx:
        def sb(name, shape, dt):
            return ctx.enter_context(nc.sbuf_tensor(name, shape, dt))

        def bank(name, dt=F32, cols=CW):
            return ctx.enter_context(nc.psum_tensor(name, [P, cols], dt))

        def sem(name):
            return ctx.enter_context(nc.semaphore(name))

        ident = sb("ident", [P, P], F32)
        ident_b = sb("ident_b", [P, P], BF16)
        mean_col = sb("mean_col", [P, 2], F32)
        mean_mat = sb("mean_mat", [P, P], F32)
        center_mat = sb("center_mat", [P, P], F32)
        conv_raw = sb("conv_raw", [P, C * KH * KW], F32)
        conv_sign = sb("conv_sign", [P, len(TAPS), 2, C], BF16)
        conv_w = sb("conv_w", [P, 2, len(TAPS), P], BF16)
        bn_rows = sb("bn_rows", [8, C], F32)
        bn_twice = sb("bn_twice", [8, 2, C], F32)
        bn_raw = sb("bn_raw", [P, 8], F32)
        bn = sb("bn", [P, 2, 2], F32)
        bn_tmp = sb("bn_tmp", [P, 2, 2], F32)
        gate_mat = sb("gate_mat", [P, 2, E], F32)
        gate_bias = sb("gate_bias", [P, E], F32)
        first_rank = sb("first_rank", [P, E], F32)
        rank_int = sb("rank_int", [P, E], mybir.dt.int32)
        up_raw = sb("up_raw", [P, 2, E, HID], F32)
        up_hi = sb("up_hi", [P, 2, E, HID], F32R)
        up_lo = sb("up_lo", [P, 2, E, HID], F32R)
        down_raw = sb("down_raw", [P, E, D], F32)
        down_hi = sb("down_hi", [P, E, D], F16)
        down_lo = sb("down_lo", [P, E, D], F16)
        largest = sb("largest", [P, 3], F32)
        largest_all = sb("largest_all", [P, 3], F32)
        scales = sb("scales", [P, 2], F32)
        unscale = sb("unscale", [P, 3], F32)
        warm = sb("warm", [P, 2], F32)
        start = sb("start", [P, 13], F32)

        x_in = sb("x_in", [P, HW], F32)
        xc = sb("xc", [P, HW], F32)
        sq = sb("sq", [P, HW], F32)
        var_eps = sb("var_eps", [P, 2, CH, TPC, 2], F32)
        rstd_wide = sb("rstd_wide", [P, CH, 2 * TPC, C], F32)
        both_eps = sb("both_eps", [P, 2], F32)
        branch1 = sb("branch1", [P, HW], F32)
        minus_half = sb("minus_half", [P, 2 * TPC], F32)
        rstd = sb("rstd", [P, 2, CH, TPC, 2], F32)
        x_ln = sb("x_ln", [P, HW], F32)
        bn_sum = sb("bn_sum", [P, HW], F32)
        sign1 = sb("sign1", [P, H + 1, W + 2], BF16)
        sign2 = sb("sign2", [P, H + 1, W + 2], BF16)
        x2 = sb("x2", [P, HW], F32)
        x2_keep = sb("x2_keep", [P, HW], F32)
        xn = sb("xn", [P, HW], F32)
        xn_hi = sb("xn_hi", [P, HW], F32R)
        xn_lo = sb("xn_lo", [P, HW], F32R)
        xs = sb("xs", [P, GROUPS, CW], F32R)
        logits = sb("logits", [P, 2 * TILES, E], F32)
        match = sb("match", [P, 2 * TILES, E], F32)
        key = sb("key", [P, 2 * TILES, E], F32)
        pick1 = sb("pick1", [P, 2 * TILES, E], F32)
        pick2 = sb("pick2", [P, 2 * TILES, E], F32)
        top = sb("top", [P, 8, 2 * TILES], F32)
        disp = sb("disp", [P, TILES, 2, E], F32)

        act_s = [sb(f"act_s{i}", [P, CW], F32) for i in range(2)]
        hidden = [sb(f"hidden{i}", [P, CW], F32) for i in range(4)]
        hidden_hi = [sb(f"hidden_hi{i}", [P, CW], F16) for i in range(RING)]
        hidden_lo = [sb(f"hidden_lo{i}", [P, CW], F16) for i in range(RING)]
        weighted = [sb(f"weighted{i}", [P, TPC, 2, D], F32) for i in range(2)]
        acc = [sb(f"acc{i}", [P, TPC, 2, D], F32) for i in range(2)]
        ffn = sb("ffn", [P, TILES, 2, D], F32)
        out_sb = [sb(f"out_sb{i}", [P, CW], F32) for i in range(CH)]

        up1 = [bank(f"up1_{i}") for i in range(2)]
        up2 = [bank(f"up2_{i}") for i in range(2)]
        down = [bank(f"down_{i}") for i in range(2)]
        misc = [bank(f"misc_{i}") for i in range(2)]

        bn_in = sem("bn_in")
        gate_in = sem("gate_in")
        conv_in = sem("conv_in")
        up_in = [sem(f"up_in{m}") for m in range(2)]
        down_in = sem("down_in")
        x_loaded = sem("x_loaded")
        stored = [sem(f"stored{c}") for c in range(CH)]
        pool_made = sem("pool_made")
        dve_made = sem("dve_made")
        taps_signed = sem("taps_signed")
        taps_turned = sem("taps_turned")
        bn_turned = sem("bn_turned")
        hi_made = sem("hi_made")
        weights_made = sem("weights_made")
        WM_LARGEST, WM_W2, WM_ALL = 4, 13, 18
        reduced = sem("reduced")
        PM_MEAN, PM_GATE, PM_BN = 7, 10, 12
        DM_CENTER, DM_ZEROS, DM_TWICE, DM_EPS, DM_ALL = 5, 8, 10, 12, 15
        center_ready, center_read = sem("center_ready"), sem("center_read")
        var_ready, var_read = sem("var_ready"), sem("var_read")
        conv1_ready, conv1_read = sem("conv1_ready"), sem("conv1_read")
        conv2_ready, conv2_read = sem("conv2_ready"), sem("conv2_read")
        center2_ready, center2_read = sem("center2_ready"), sem("center2_read")
        var2_ready, var2_read = sem("var2_ready"), sem("var2_read")
        norm_ready, norm2_ready = sem("norm_ready"), sem("norm2_ready")
        gate_ready, gate_read = sem("gate_ready"), sem("gate_read")
        back_ready = [sem(f"back_ready{c}") for c in range(CH)]
        back_read = [sem(f"back_read{c}") for c in range(CH)]
        rstd_ready, rstd2_ready = sem("rstd_ready"), sem("rstd2_ready")
        powed = sem("powed")
        sign1_ready = sem("sign1_ready")
        x_ln_ready = sem("x_ln_ready")
        relu1_ready = sem("relu1_ready")
        relu_ready = sem("relu_ready")
        x2_ready = sem("x2_ready")
        x2_kept = sem("x2_kept")
        xn_ready = sem("xn_ready")
        xs_hi_ready = sem("xs_hi_ready")
        xs_lo_ready = sem("xs_lo_ready")
        xs_ready = [sem(f"xs_ready{c}") for c in range(CH)]
        gap_ready = sem("gap_ready")
        tanh_ready = sem("tanh_ready")
        disp_done = sem("disp_done")
        route_link = sem("route_link")
        up1_ready = sem("up1_ready")
        up2_ready = sem("up2_ready")
        silu_done = sem("silu_done")
        hidden_done = sem("hidden_done")
        hi_done = sem("hi_done")
        lo_done = [sem(f"lo_done{i}") for i in range(2)]
        down_done = sem("down_done")
        weighted_done = sem("weighted_done")
        added = sem("added")
        ffn_done = sem("ffn_done")

        block = ctx.enter_context(nc.Block())

        def turned(eng, front, slot, finish):
            front()
            for k in range(TURN):
                slot(k, 0, False)
            if PAIRS > 1:
                with eng.Fori(0, PAIRS - 1) as p:
                    for k in range(TURN, SLOTS):
                        slot(k, p, True)
                    for k in range(TURN):
                        slot(k, p + 1, False)
            for k in range(TURN, SLOTS):
                slot(k, PAIRS - 1, False)
            finish()

        def front_steps(engine):
            return [s for k in sorted(PLAN[engine]) if k < CATCH_UP[0][0] for s in PLAN[engine][k]
                    if s[0] not in ("residual", "back")]

        def steps_beside(engine, k, p, more):
            if isinstance(p, int) and p == 0 and k < TURN:
                for at in range(*CATCH_UP[k]):
                    yield from ((*step, 0) for step in PLAN[engine].get(at, []) if step[0] != "back")
                return
            for name, part in PLAN[engine].get(k, []):
                if name in ("residual", "back"):
                    yield name, part, p
                elif more:
                    yield name, part, p + 1
            for name, part in PLAN[engine].get(k + SLOTS, []):
                if name != "back":
                    yield name, part, p
                else:
                    yield name, part, p - 1

        def before(n, lag, total, p):
            if n >= lag:
                return n - lag, p
            return None if isinstance(p, int) else (n - lag + total, p - 1)

        def low_made(u, p):
            return lo_done[u % 2], UNITS // 2 * p + u // 2 + 3

        def cols(c):
            return slice(c * CW, (c + 1) * CW)

        def rows_of(c):
            return slice(c * 2 * TPC, (c + 1) * 2 * TPC)

        @block.sync
        def _(sp):
            sp.dma_start(x_in[:, :], x_pairs[0]).then_inc(x_loaded, 16)
            sp.dma_start(conv_raw[0:C, :], w1.rearrange("o c i j -> o (c i j)")).then_inc(conv_in, 16)
            sp.dma_start(conv_raw[C:P, :], w2.rearrange("o c i j -> o (c i j)")).then_inc(conv_in, 16)
            for i, v in enumerate((gamma1, beta1, mean1, var1, gamma2, beta2, mean2, var2)):
                sp.dma_start(bn_rows[i:i + 1, :], v.rearrange("(one c) -> one c", one=1)).then_inc(bn_in, 16)
            for m, w in enumerate((ffn_w1, ffn_w2)):
                for half in range(2):
                    sp.dma_start(up_raw[half * D:(half + 1) * D, m, :, :],
                                 w.rearrange("e d h -> d e h")).then_inc(up_in[m], 16)
            sp.dma_start(down_raw[:, :, :], ffn_w3.rearrange("e h d -> h e d")).then_inc(down_in, 16)
            sp.wait_ge(pool_made, PM_GATE)
            for half in range(2):
                sp.dma_start(gate_mat[half * D:(half + 1) * D, half, :], gate_w).then_inc(gate_in, 16)
            sp.dma_start(gate_bias[:, :], gate_b.partition_broadcast(P)).then_inc(gate_in, 16)

            def store(c, p):
                sp.wait_ge(back_read[c], p + 2)
                sp.dma_start(out_pairs[p, :, cols(c)], out_sb[c][:, :]).then_inc(stored[c], 16)

            def load(q):
                sp.wait_ge(x2_ready, CH * q)
                sp.dma_start(x_in[:, :], x_pairs[q]).then_inc(x_loaded, 16)

            def stack(c, q):
                sp.wait_ge(xs_lo_ready, CH * q + c + 1)
                for image in range(2):
                    rows, other = slice(image * D, (image + 1) * D), slice((1 - image) * D, (2 - image) * D)
                    for half, part in ((rows, xn_hi), (other, xn_lo)):
                        sp.dma_start(xs[half, 2 * c + image, :].bitcast(F32), part[rows, cols(c)].bitcast(F32))\
                            .then_inc(xs_ready[c], 16)

            load(1)
            for c in range(CH):
                stack(c, 0)
            with sp.Fori(0, PAIRS - 2) as p:
                load(p + 2)
                stack(0, p + 1)
                for c in range(CH):
                    store(c, p)
                stack(1, p + 1)
            stack(0, PAIRS - 1)
            for c in range(CH):
                store(c, PAIRS - 2)
            stack(1, PAIRS - 1)
            for c in range(CH):
                store(c, PAIRS - 1)
            for c in range(CH):
                sp.wait_ge(stored[c], 16 * PAIRS + 16)

        @block.gpsimd
        def _(pool):
            pool.memset(ident[:, :], 0.0).then_inc(pool_made, 1)
            pool.memset(mean_mat[:, :], 0.0).then_inc(pool_made, 1)
            pool.wait_ge(pool_made, 2)
            pool.affine_select(out=ident[:, :], in_=ident[:, :], compare_op=ALU.not_equal, fill=1.0,
                               base=0, pattern=[[-1, P]], channel_multiplier=1).then_inc(pool_made, 1)
            for half in range(2):
                pool.wait_ge(pool_made, 3 + half)
                pool.memset(mean_mat[half * C:(half + 1) * C, half * C:(half + 1) * C], 1.0 / C)\
                    .then_inc(pool_made, 1)
            pool.wait_ge(pool_made, 5)
            pool.memset(mean_col[:, :], 0.0).then_inc(pool_made, 1)
            pool.memset(minus_half[:, :], -0.5).then_inc(pool_made, 1)
            for half in range(2):
                pool.wait_ge(pool_made, PM_MEAN + half)
                pool.memset(mean_col[half * C:(half + 1) * C, half:half + 1], 1.0 / C).then_inc(pool_made, 1)
            pool.wait_ge(pool_made, PM_MEAN + 2)
            pool.memset(gate_mat[:, :, :], 0.0).then_inc(pool_made, 1)
            pool.iota(rank_int[:, :], [[-1, E]], base=E, channel_multiplier=0).then_inc(pool_made, 1)
            pool.wait_ge(dve_made, DM_EPS)
            pool.tensor_tensor(bn_tmp[:, :, 0:1], bn_tmp[:, :, 0:1],
                               minus_half[:, 0:2].unsqueeze(2), ALU.pow).then_inc(pool_made, 1)

            def step(name, c, q):
                if name in ("var", "var2"):
                    n = 0 if name == "var" else 1
                    pool.wait_ge((var_read, var2_read)[n], CH * q + c + 1)
                    pool.tensor_tensor(rstd[:, n, c, :, :], var_eps[:, n, c, :, :],
                                       minus_half[:, :].rearrange("p (t a) -> p t a", a=2), ALU.pow).then_inc(powed, 1)
                elif name == "x2":
                    pool.wait_ge(x2_kept, CH * q)
                    pool.wait_ge(relu_ready, CH * q + c + 1)
                    pool.tensor_tensor(x2[:, cols(c)], x_in[:, cols(c)], bn_sum[:, cols(c)], ALU.add)\
                        .then_inc(x2_ready, 1)

            def front():
                for at in front_steps("Pool"):
                    step(*at, 0)
                    if at == ("var", 0):
                        pool.wait_ge(weights_made, WM_LARGEST)
                        pool.partition_all_reduce(largest_all[:, :], largest[:, :], P, bass.bass_isa.ReduceOp.max)\
                            .then_inc(reduced, 1)

            def low_part(u, p):
                pool.wait_ge(hi_done, UNITS * p + u + 1)
                pool.tensor_tensor(hidden_lo[u % RING][:, :], hidden[u % 4][:, :], hidden_hi[u % RING][:, :],
                                   ALU.subtract).then_inc(lo_done[0], 1)

            def add_up(k, p):
                group, ep = k // EP, k % EP
                if ep > 0:
                    n = (EP - 1) * group + ep - 1
                    pool.wait_ge(weighted_done, SLOTS * p + k + 3)
                    if ep > 1:
                        pool.wait_ge(added, ADDS * p + n + 2)
                    pool.tensor_tensor(acc[group % 2][:, :, :, :], acc[group % 2][:, :, :, :],
                                       weighted[n % 2][:, :, :, :], ALU.add).then_inc(added, 1)
                if ep == EP - 1:
                    chunk, image = group // 2, group % 2
                    pool.wait_ge(back_ready[chunk], p + 1)
                    pool.wait_ge(added, ADDS * p + (EP - 1) * (group + 1) + 2)
                    pool.tensor_tensor(ffn[:, chunk * TPC:(chunk + 1) * TPC, image, :],
                                       acc[group % 2][:, :, 0, :], acc[group % 2][:, :, 1, :], ALU.add)\
                        .then_inc(ffn_done, 1)

            def slot(k, p, more):
                if at := before(2 * k, LO_LAG, UNITS, p):
                    low_part(*at)
                if at := before(k, WEIGH_LAG, SLOTS, p):
                    add_up(*at)
                for at in steps_beside("Pool", k, p, more):
                    step(*at)

            def finish():
                low_part(UNITS - 2, PAIRS - 1)
                for k in range(SLOTS - WEIGH_LAG, SLOTS):
                    add_up(k, PAIRS - 1)

            turned(pool, front, slot, finish)

        @block.scalar
        def _(act):
            act.wait_ge(dve_made, 1)
            act.activation(warm[:, 1:2], warm[:, 0:1], ACT.Silu).then_inc(silu_done, 2)
            act.wait_ge(conv_in, 32)
            for half in range(2):
                act.activation(conv_sign[:, :, half, :],
                               conv_raw[:, :].rearrange("p (c t) -> p t c", t=len(TAPS)), ACT.Sign)\
                    .then_inc(taps_signed, 1)

            def make_hi(part):
                if part == 0:
                    act.wait_ge(up_in[0], 32)
                else:
                    act.wait_ge(weights_made, WM_W2)
                act.activation(up_hi[:, part, :, :], up_raw[:, part, :, :], ACT.Copy).then_inc(hi_made, 1)
                if part == 1:
                    act.activation(down_hi[:, :, :], down_raw[:, :, :], ACT.Copy).then_inc(hi_made, 1)

            def step(name, c, q):
                if name == "residual":
                    act.wait_ge(back_read[c], q + 1)
                    act.wait_ge(x2_ready, CH * (q + 1))
                    act.activation(x2_keep[:, cols(c)], x2[:, cols(c)], ACT.Copy).then_inc(x2_kept, 1)
                elif name in ("wide", "wide2"):
                    n = 0 if name == "wide" else 1
                    act.wait_ge(powed, 2 * CH * q + CH * n + c + 1)
                    act.activation(rstd_wide[:, c, :, :],
                                   rstd[:, n, c, :, :].rearrange("p t a -> p (t a)").unsqueeze(2)
                                   .to_broadcast([P, 2 * TPC, C]), ACT.Copy)\
                        .then_inc((rstd_ready, rstd2_ready)[n], 1)
                elif name == "square":
                    act.wait_ge(center_ready, CH * q + c + 1)
                    act.activation(sq[:, cols(c)], misc[c][:, :], ACT.Square)
                elif name == "sign":
                    act.activation(sign1[:, c * ROWS:(c + 1) * ROWS, 1:W + 1],
                                   misc[c][:, :].rearrange("p (h w) -> p h w", w=W), ACT.Sign)\
                        .then_inc(sign1_ready, 1)
                elif name == "copy":
                    act.wait_ge(xn_ready, CH * q)
                    act.activation(xc[:, cols(c)], misc[c][:, :], ACT.Copy).then_inc(center_read, 1)
                elif name == "relu":
                    act.wait_ge(conv2_read, CH * q + c + 1)
                    act.activation(bn_sum[:, cols(c)], bn_sum[:, cols(c)], ACT.Relu, bias=bn[:, 1, 1:2])\
                        .then_inc(relu_ready, 1)
                elif name == "square2":
                    act.wait_ge(center2_ready, CH * q + c + 1)
                    act.activation(sq[:, cols(c)], misc[c][:, :], ACT.Square)
                elif name in ("var", "var2"):
                    n = 0 if name == "var" else 1
                    act.wait_ge((var_ready, var2_ready)[n], CH * q + c + 1)
                    act.activation(var_eps[:, n, c, :, :], misc[c][:, 0:2 * TPC].rearrange("p (t a) -> p t a", a=2),
                                   ACT.Identity, bias=both_eps[:, n:n + 1]).then_inc((var_read, var2_read)[n], 1)
                elif name == "conv1":
                    act.wait_ge(conv1_ready, CH * q + c + 1)
                    act.activation(branch1[:, cols(c)], misc[c][:, :], ACT.Relu, scale=bn[:, 0, 0:1], bias=bn[:, 0, 1:2])\
                        .then_inc(relu1_ready, 1)
                    act.wait_ge(relu1_ready, CH * q + c + 1)
                    act.activation(sign2[:, c * ROWS:(c + 1) * ROWS, 1:W + 1],
                                   branch1[:, cols(c)].rearrange("p (h w) -> p h w", w=W), ACT.Sign)\
                        .then_inc(conv1_read, 1)
                elif name == "copy2":
                    act.activation(xc[:, cols(c)], misc[c][:, :], ACT.Copy).then_inc(center2_read, 1)
                elif name == "split":
                    act.wait_ge(xn_ready, CH * q + c + 1)
                    if c == 0 and not isinstance(q, int):
                        act.wait_ge(up2_ready, UNITS * (q - 1) + 2 * E)
                    act.activation(xn_hi[:, cols(c)], xn[:, cols(c)], ACT.Copy).then_inc(xs_hi_ready, 1)
                elif name == "tanh":
                    rows = rows_of(c)
                    act.wait_ge(gap_ready, CH * q + c + 1)
                    act.activation(top[:, 5, rows], top[:, 4, rows], ACT.Tanh, scale=0.5).then_inc(tanh_ready, 1)

            def front():
                act.wait_ge(dve_made, DM_ZEROS)
                for at in front_steps("ScalarE"):
                    if at == ("conv1", 0):
                        act.wait_ge(dve_made, DM_ALL)
                    step(*at, 0)
                    if at == ("var", 1):
                        make_hi(0)
                    if at == ("conv1", 1):
                        make_hi(1)

            def high_part(u, p):
                act.wait_ge(hidden_done, UNITS * p + u + 3)
                act.wait_ge(down_done, UNITS * p + u + 1)
                act.activation(hidden_hi[u % RING][:, :], hidden[u % 4][:, :], ACT.Copy).then_inc(hi_done, 1)

            def slot(k, p, more):
                for u in (2 * k, 2 * k + 1):
                    act.wait_ge(up1_ready, UNITS * p + u + 1)
                    act.wait_ge(hidden_done, UNITS * p + u + 1)
                    act.activation(act_s[u % 2][:, :], up1[u % 2][:, :], ACT.Silu).then_inc(silu_done, 1)
                    if at := before(u, HI_LAG, UNITS, p):
                        high_part(*at)
                for at in steps_beside("ScalarE", k, p, more):
                    step(*at)

            turned(act, front, slot, lambda: high_part(UNITS - 1, PAIRS - 1))

        @block.tensor
        def _(pe):
            pe.wait_ge(dve_made, DM_CENTER)

            def transpose_taps():
                pe.wait_ge(taps_signed, 2)
                turned_taps = up1[0][:, :].bitcast(BF16)
                for t in range(len(TAPS)):
                    last = pe.transpose(turned_taps[:, t * P:(t + 1) * P],
                                        conv_sign[:, t, :, :].rearrange("p a c -> p (a c)"), ident_b[:, :])
                last.then_inc(taps_turned, 1)

            def transpose_batch_norms():
                pe.wait_ge(dve_made, DM_TWICE)
                pe.transpose(down[0][:, 0:8], bn_twice[:, :, :].rearrange("v a c -> v (a c)"), ident[0:8, 0:8])\
                    .then_inc(bn_turned, 1)


            def conv_half(half, which, image):
                c, taps = half // 2, len(TAPS) // 2
                for t in range(half % 2 * taps, (half % 2 + 1) * taps):
                    i, j = TAPS[t]
                    last = pe.matmul(misc[c][:, :], conv_w[:, which, t, :],
                                     image[:, c * ROWS + i:(c + 1) * ROWS + i, j:j + W],
                                     start=(t == 0), stop=(t == len(TAPS) - 1))
                return last

            def center_half(half, source):
                c, width = half // 2, CW // 2
                at = half % 2 * width
                return pe.matmul(misc[c][:, at:at + width], center_mat[:, :],
                                 source[:, c * CW + at:c * CW + at + width], start=True, stop=True)

            def step(name, c, q):
                if name == "center":
                    half, c = c, c // 2
                    if half % 2 == 0:
                        pe.wait_ge(x_loaded, 16 * (q + 1))
                        if not isinstance(q, int):
                            pe.wait_ge(gate_read, CH * q)
                            pe.wait_ge(back_read[c], q)
                    last = center_half(half, x_in)
                    if half % 2 == 1:
                        last.then_inc(center_ready, 1)
                elif name in ("var", "var2"):
                    n = 0 if name == "var" else 1
                    pe.wait_ge((center_read, center2_read)[n], CH * q + c + 1)
                    for t in range(TPC):
                        last = pe.matmul(misc[c][:, 2 * t:2 * t + 2],
                                         sq[:, c * CW + t * P:c * CW + (t + 1) * P], mean_col[:, :],
                                         start=True, stop=True)
                    last.then_inc((var_ready, var2_ready)[n], 1)
                elif name in ("norm", "norm2"):
                    n = 0 if name == "norm" else 1
                    pe.wait_ge((conv1_read, var2_read)[n], CH * q + c + 1)
                    if name == "norm2" and c == 0:
                        pe.wait_ge(back_read[0], q + 1)
                    pe.wait_ge((rstd_ready, rstd2_ready)[n], CH * q + c + 1)
                    for t in range(TPC):
                        last = pe.transpose(misc[c][:, t * P:(t + 1) * P],
                                            rstd_wide[:, c, 2 * t:2 * t + 2, :].rearrange("p a c -> p (a c)"),
                                            ident[:, :])
                    last.then_inc((norm_ready, norm2_ready)[n], 1)
                elif name == "conv1":
                    if c % 2 == 0:
                        pe.wait_ge(var_read, CH * q + c // 2 + 1)
                        pe.wait_ge(sign1_ready, CH * (q + 1))
                    last = conv_half(c, 0, sign1)
                    if c % 2 == 1:
                        last.then_inc(conv1_ready, 1)
                elif name == "conv2":
                    if c % 2 == 0:
                        pe.wait_ge(conv1_read, CH * (q + 1))
                        pe.wait_ge(x_ln_ready, CH * q + c // 2 + 1)
                    last = conv_half(c, 1, sign2)
                    if c % 2 == 1:
                        last.then_inc(conv2_ready, 1)
                elif name == "center2":
                    half, c = c, c // 2
                    if half % 2 == 0:
                        pe.wait_ge(conv2_read, CH * q + c + 1)
                        pe.wait_ge(x2_ready, CH * q + c + 1)
                    last = center_half(half, x2)
                    if half % 2 == 1:
                        last.then_inc(center2_ready, 1)
                elif name == "gate":
                    pe.wait_ge(xn_ready, CH * q + c + 1)
                    for t in range(TPC):
                        j = c * TPC + t
                        last = pe.matmul(misc[c][:, t * 2 * E:(t + 1) * 2 * E], xn[:, j * P:(j + 1) * P],
                                         gate_mat[:, :, :].rearrange("p a e -> p (a e)"), start=True, stop=True)
                    last.then_inc(gate_ready, 1)
                elif name == "back":
                    pe.wait_ge(ffn_done, GROUPS * q + 2 * (c + 1) + 2)
                    pe.wait_ge((var2_read, gate_read)[c],
                               CH * PAIRS if isinstance(q, int) else CH * (q + 1) + c + 1)
                    for t in range(TPC):
                        last = pe.transpose(misc[c][:, t * P:(t + 1) * P],
                                            ffn[:, c * TPC + t, :, :].rearrange("p a d -> p (a d)"), ident[:, :])
                    last.then_inc(back_ready[c], 1)

            def front():
                for at in front_steps("TensorE"):
                    if at == ("var", 0):
                        pe.wait_ge(pool_made, PM_GATE)
                    if at == ("conv1", 0):
                        pe.wait_ge(weights_made, 1)
                    if at == ("gate", 0):
                        pe.wait_ge(gate_in, 48)
                    step(*at, 0)
                    if at == ("center", 2):
                        transpose_taps()
                    if at == ("center", 3):
                        transpose_batch_norms()

            def down_product(u, p):
                k, e = u // 2, u % E
                pe.wait_ge(*low_made(u, p))
                if u % 2 == 0:
                    pe.wait_ge(weighted_done, SLOTS * p + k + 1)
                parts = ((hidden_hi, down_hi), (hidden_hi, down_lo), (hidden_lo, down_hi))
                for t in range(TPC):
                    for n, (h, w) in enumerate(parts):
                        last = pe.matmul(down[k % 2][:, (2 * t + u % 2) * D:(2 * t + u % 2 + 1) * D],
                                         h[u % RING][:, t * P:(t + 1) * P], w[:, e, :],
                                         start=(n == 0), stop=(n == len(parts) - 1))
                last.then_inc(down_done, 1)

            def slot(k, p, more):
                group = k // EP
                if k == 0 and isinstance(p, int):
                    pe.wait_ge(weights_made, WM_ALL)
                if k % (2 * EP) == 0:
                    pe.wait_ge(xs_ready[group // 2], 64 * (p + 1))
                for u in (2 * k, 2 * k + 1):
                    e = u % E
                    for m, (banks, free, ready) in enumerate(((up1, silu_done, up1_ready),
                                                              (up2, hidden_done, up2_ready))):
                        pe.wait_ge(free, UNITS * p + u + 1)
                        pe.matmul(banks[u % 2][:, :], up_hi[:, m, e, :], xs[:, group, :], start=True, stop=False)
                        pe.matmul(banks[u % 2][:, :], up_lo[:, m, e, :], xs[:, group, :], start=False, stop=True)\
                            .then_inc(ready, 1)
                for u in (2 * k, 2 * k + 1):
                    if at := before(u, DOWN_LAG, UNITS, p):
                        down_product(*at)
                for at in steps_beside("TensorE", k, p, more):
                    step(*at)

            def finish():
                for u in range(UNITS - DOWN_LAG, UNITS):
                    down_product(u, PAIRS - 1)
                step("back", 1, PAIRS - 1)

            turned(pe, front, slot, finish)

        @block.vector
        def _(dve):
            dve.memset(warm[:, :], 0.0).then_inc(dve_made, 1)
            for i, (free, count) in enumerate(((hidden_done, 2), (down_done, RING), (added, 2),
                                               (lo_done[0], 2), (lo_done[1], 2),
                                               (weighted_done, 2), (ffn_done, 2),
                                               (back_ready[0], 1), (back_ready[1], 1), (back_read[0], 1),
                                               (back_read[1], 1), (stored[0], 16), (stored[1], 16))):
                dve.memset(start[:, i:i + 1], 0.0).then_inc(free, count)
            dve.wait_ge(pool_made, PM_MEAN)
            dve.tensor_copy(ident_b[:, :], ident[:, :]).then_inc(dve_made, 1)
            dve.tensor_tensor(center_mat[:, :], ident[:, :], mean_mat[:, :], ALU.subtract)\
                .then_inc(dve_made, 1)
            for n, eps in enumerate((EPS_CONV_LN, EPS_TOKEN_LN)):
                dve.memset(both_eps[:, n:n + 1], eps).then_inc(dve_made, 1)
            for zeroed in (sign1[:, :, :], sign2[:, :, :], conv_w[:, :, :, :]):
                dve.memset(zeroed, 0.0).then_inc(dve_made, 1)
            dve.wait_ge(pool_made, PM_GATE + 1)
            dve.tensor_copy(first_rank[:, :], rank_int[:, :]).then_inc(dve_made, 1)

            raw = bn_raw[:, :].rearrange("p (k v) -> p k v", k=2)

            def batch_norms(part):
                if part == 0:
                    dve.wait_ge(bn_in, 16 * 8)
                    dve.tensor_copy(bn_twice[:, :, :], bn_rows[:, :].unsqueeze(1).to_broadcast([8, 2, C]))\
                        .then_inc(dve_made, 1)
                    return
                if part == 1:
                    dve.wait_ge(bn_turned, 1)
                    dve.tensor_copy(bn_raw[:, :], down[0][:, 0:8]).then_inc(dve_made, 1)
                    dve.wait_ge(dve_made, DM_TWICE + 1)
                    dve.tensor_scalar(bn_tmp[:, :, 0:1], raw[:, :, 3:4], EPS_BN, None, ALU.add)\
                        .then_inc(dve_made, 1)
                    return
                dve.wait_ge(pool_made, PM_BN)
                dve.tensor_tensor(bn[:, :, 0:1], bn_tmp[:, :, 0:1], raw[:, :, 0:1], ALU.mult).then_inc(dve_made, 1)
                dve.wait_ge(dve_made, DM_EPS + 1)
                dve.tensor_tensor(bn_tmp[:, :, 1:2], raw[:, :, 2:3], bn[:, :, 0:1], ALU.mult).then_inc(dve_made, 1)
                dve.wait_ge(dve_made, DM_EPS + 2)
                dve.tensor_tensor(bn[:, :, 1:2], raw[:, :, 1:2], bn_tmp[:, :, 1:2], ALU.subtract).then_inc(dve_made, 1)
                dve.wait_ge(dve_made, DM_ALL)

            def place_taps():
                dve.wait_ge(taps_turned, 1)
                dve.wait_ge(dve_made, DM_ZEROS)
                turned_taps = up1[0][:, :].bitcast(BF16)[:, 0:len(TAPS) * P]
                turned_taps = turned_taps.rearrange("p (t k o) -> p t k o", t=len(TAPS), k=2)
                for half in range(2):
                    rows = slice(half * C, (half + 1) * C)
                    for k in range(2):
                        last = dve.tensor_copy(conv_w[rows, k, :, rows], turned_taps[rows, :, k, :])
                last.then_inc(weights_made, 1)

            def find_largest(m):
                if m < 2:
                    dve.wait_ge(up_in[m], 32)
                    source = up_raw[:, m, :, :].rearrange("p e h -> p (e h)")
                else:
                    dve.wait_ge(down_in, 16)
                    source = down_raw[:, :, :].rearrange("p e d -> p (e d)")
                dve.tensor_reduce(largest[:, m:m + 1], source, AX.X, ALU.max, apply_absolute_value=True)\
                    .then_inc(weights_made, 1)

            def scale_weights():
                def then(ins, count):
                    ins.then_inc(weights_made, 1)
                    dve.wait_ge(weights_made, count)
                dve.wait_ge(reduced, 1)
                then(dve.tensor_scalar(largest[:, :], largest_all[:, :], LEAST_WEIGHT, None, ALU.max), 5)
                then(dve.tensor_tensor(largest[:, 1:2], largest[:, 0:1], largest[:, 1:2], ALU.mult), 6)
                then(dve.reciprocal(scales[:, :], largest[:, 1:3]), 7)
                then(dve.tensor_scalar(scales[:, 0:1], scales[:, 0:1], 2.0 ** 15 / D ** 2, None, ALU.mult), 8)
                then(dve.tensor_scalar(scales[:, 1:2], scales[:, 1:2], 2.0 ** 14, None, ALU.mult), 9)
                then(dve.tensor_scalar(scales[:, :].bitcast(U32), scales[:, :].bitcast(U32), EXPONENT_BITS, None,
                                       ALU.bitwise_and), 10)
                then(dve.tensor_tensor(unscale[:, 0:1], scales[:, 0:1], scales[:, 1:2], ALU.mult), 11)
                dve.tensor_scalar(down_raw[:, :, :], down_raw[:, :, :], scales[:, 1:2], None, ALU.mult)\
                    .then_inc(weights_made, 1)
                dve.tensor_scalar(up_raw[:, 1, :, :], up_raw[:, 1, :, :], scales[:, 0:1], None, ALU.mult)\
                    .then_inc(weights_made, 1)

            def make_lo(m):
                dve.wait_ge(hi_made, m + 1)
                if m < 2:
                    dve.tensor_tensor(up_lo[:, m, :, :], up_raw[:, m, :, :], up_hi[:, m, :, :].bitcast(F32),
                                      ALU.subtract).then_inc(weights_made, 1)
                    return
                dve.tensor_tensor(down_lo[:, :, :], down_raw[:, :, :], down_hi[:, :, :], ALU.subtract)\
                    .then_inc(weights_made, 1)
                dve.reciprocal(unscale[:, 1:2], unscale[:, 0:1]).then_inc(weights_made, 1)
                dve.wait_ge(weights_made, WM_ALL - 1)
                dve.tensor_scalar(unscale[:, 2:3], unscale[:, 1:2], -0.5, None, ALU.mult).then_inc(weights_made, 1)
                dve.wait_ge(weights_made, WM_ALL)
                dve.tensor_scalar(unscale[:, 1:2], unscale[:, 1:2], 0.5, None, ALU.mult).then_inc(weights_made, 1)
                dve.wait_ge(weights_made, WM_ALL + 1)

            LINKS = 15

            def spread(a):
                return a.unsqueeze(2).to_broadcast([P, 2 * TPC, E])

            def ranks():
                return first_rank[:, :].unsqueeze(1).to_broadcast([P, 2 * TPC, E])

            def pick_first(part, best, pick, n, at):
                rows = rows_of(n[1])
                done = LINKS * (CH * n[0] + n[1]) + at
                if part == 0:
                    dve.tensor_reduce(top[:, best, rows], logits[:, rows, :], AX.X, ALU.max).then_inc(route_link, 1)
                    dve.wait_ge(route_link, done)
                    dve.tensor_tensor(match[:, rows, :], logits[:, rows, :], spread(top[:, best, rows]),
                                      ALU.is_equal).then_inc(route_link, 1)
                elif part == 1:
                    dve.wait_ge(route_link, done + 1)
                    dve.tensor_tensor(key[:, rows, :], match[:, rows, :], ranks(), ALU.mult).then_inc(route_link, 1)
                    dve.wait_ge(route_link, done + 2)
                    dve.tensor_reduce(top[:, 7, rows], key[:, rows, :], AX.X, ALU.max).then_inc(route_link, 1)
                else:
                    dve.wait_ge(route_link, done + 3)
                    dve.tensor_tensor(pick[:, rows, :], key[:, rows, :], spread(top[:, 7, rows]), ALU.is_equal)\
                        .then_inc(route_link, 1)

            def route(part, c, q):
                rows = rows_of(c)
                done = LINKS * (CH * q + c)
                if part < 3:
                    if part == 0:
                        dve.wait_ge(gate_read, CH * q + c + 1)
                    pick_first(part, 0, pick1, (q, c), 1)
                    if part == 2:
                        dve.wait_ge(route_link, done + 5)
                        dve.scalar_tensor_tensor(out=logits[:, rows, :], in0=pick1[:, rows, :], scalar=MASKED,
                                                 in1=logits[:, rows, :], op0=ALU.mult, op1=ALU.add)\
                            .then_inc(route_link, 1)
                elif part < 6:
                    dve.wait_ge(route_link, done + 6)
                    pick_first(part - 3, 1, pick2, (q, c), 7)
                    if part == 3:
                        dve.tensor_tensor(top[:, 4, rows], top[:, 0, rows], top[:, 1, rows], ALU.subtract)\
                            .then_inc(gap_ready, 1)
                elif part == 6:
                    dve.wait_ge(tanh_ready, CH * q + c + 1)
                    dve.tensor_scalar(top[:, 2, rows], top[:, 5, rows], unscale[:, 1:2], unscale[:, 1:2],
                                      ALU.mult, ALU.add).then_inc(route_link, 1)
                    dve.tensor_scalar(top[:, 3, rows], top[:, 5, rows], unscale[:, 2:3], unscale[:, 1:2],
                                      ALU.mult, ALU.add).then_inc(route_link, 1)
                else:
                    dve.wait_ge(route_link, done + 13)
                    dve.tensor_tensor(pick1[:, rows, :], pick1[:, rows, :], spread(top[:, 2, rows]), ALU.mult)\
                        .then_inc(route_link, 1)
                    dve.tensor_tensor(pick2[:, rows, :], pick2[:, rows, :], spread(top[:, 3, rows]), ALU.mult)\
                        .then_inc(route_link, 1)

            def dispatch(c, q):
                rows = rows_of(c)
                dve.wait_ge(route_link, LINKS * (CH * q + c + 1))
                dve.wait_ge(weighted_done, SLOTS * q + 2 * EP * c + 2)
                dve.tensor_tensor(disp[:, :, :, :].rearrange("p t a e -> p (t a) e")[:, rows, :],
                                  pick1[:, rows, :], pick2[:, rows, :], ALU.add).then_inc(disp_done, 1)

            def step(name, c, q):
                if name == "norm":
                    dve.wait_ge(norm_ready, CH * q + c + 1)
                    dve.tensor_tensor(x_ln[:, cols(c)], misc[c][:, :], xc[:, cols(c)], ALU.mult)\
                        .then_inc(x_ln_ready, 1)
                elif name == "norm2":
                    dve.wait_ge(norm2_ready, CH * q + c + 1)
                    dve.tensor_tensor(xn[:, cols(c)], misc[c][:, :], xc[:, cols(c)], ALU.mult)\
                        .then_inc(xn_ready, 1)
                elif name == "conv2":
                    dve.wait_ge(conv2_ready, CH * q + c + 1)
                    dve.wait_ge(x_ln_ready, CH * q + c + 1)
                    dve.scalar_tensor_tensor(out=bn_sum[:, cols(c)], in0=misc[c][:, :], scalar=bn[:, 1, 0:1],
                                             in1=x_ln[:, cols(c)], op0=ALU.mult, op1=ALU.add)\
                        .then_inc(conv2_read, 1)
                elif name == "gate":
                    rows = rows_of(c)
                    dve.wait_ge(gate_ready, CH * q + c + 1)
                    dve.tensor_tensor(logits[:, rows, :],
                                      misc[c][:, 0:2 * TPC * E].rearrange("p (t e) -> p t e", e=E),
                                      gate_bias[:, :].unsqueeze(1).to_broadcast([P, 2 * TPC, E]), ALU.add)\
                        .then_inc(gate_read, 1)
                elif name == "split":
                    dve.wait_ge(xs_hi_ready, CH * q + c + 1)
                    dve.tensor_tensor(xn_lo[:, cols(c)], xn[:, cols(c)], xn_hi[:, cols(c)].bitcast(F32),
                                      ALU.subtract).then_inc(xs_lo_ready, 1)
                elif name == "route":
                    route(c % ROUTE_PARTS, c // ROUTE_PARTS, q)
                elif name == "back":
                    dve.wait_ge(back_ready[c], q + 2)
                    dve.wait_ge(x2_kept, CH * q + c + 1)
                    dve.wait_ge(stored[c], 16 * q + 16)
                    dve.tensor_tensor(out_sb[c][:, :], misc[c][:, :], x2_keep[:, cols(c)], ALU.add)\
                        .then_inc(back_read[c], 1)

            def front():
                beside = {("norm", 0): lambda: (scale_weights(), make_lo(0)),
                          ("norm", 1): lambda: (make_lo(1), make_lo(2))}
                batch_norms(0)
                place_taps()
                batch_norms(1)
                batch_norms(2)
                for m in range(3):
                    find_largest(m)
                for at in front_steps("VectorE"):
                    if at == ("gate", 0):
                        dve.wait_ge(gate_in, 48)
                    step(*at, 0)
                    if at in beside:
                        beside[at]()

            def weigh(k, p):
                group, ep = k // EP, k % EP
                chunk, image = group // 2, group % 2
                dve.wait_ge(down_done, UNITS * p + 2 * k + 2 + RING)
                weights = disp[:, chunk * TPC:(chunk + 1) * TPC, image, 2 * ep:2 * ep + 2]
                weights = weights.unsqueeze(3).to_broadcast([P, TPC, 2, D])
                if k % (2 * EP) == 0:
                    dve.wait_ge(disp_done, CH * p + chunk + 1)
                if ep == 0:
                    dve.wait_ge(ffn_done, GROUPS * p + group + 1)
                    dst = acc[group % 2]
                else:
                    n = (EP - 1) * group + ep - 1
                    dve.wait_ge(added, ADDS * p + n + 1)
                    dst = weighted[n % 2]
                dve.tensor_tensor(dst[:, :, :, :], down[k % 2][:, :].rearrange("p (t a d) -> p t a d", a=2, d=D),
                                  weights, ALU.mult).then_inc(weighted_done, 1)

            def low_part(u, p):
                dve.wait_ge(hi_done, UNITS * p + u + 1)
                dve.tensor_tensor(hidden_lo[u % RING][:, :], hidden[u % 4][:, :], hidden_hi[u % RING][:, :],
                                  ALU.subtract).then_inc(lo_done[1], 1)

            def slot(k, p, more):
                if at := before(k, WEIGH_LAG, SLOTS, p):
                    weigh(*at)
                for u in (2 * k, 2 * k + 1):
                    dve.wait_ge(silu_done, UNITS * p + u + 3)
                    dve.wait_ge(up2_ready, UNITS * p + u + 1)
                    dve.wait_ge(*low_made(u - 4, p))
                    dve.tensor_tensor(hidden[u % 4][:, :], act_s[u % 2][:, :], up2[u % 2][:, :], ALU.mult)\
                        .then_inc(hidden_done, 1)
                    if u % 2 == 1:
                        if at := before(u, LO_LAG, UNITS, p):
                            low_part(*at)
                for at in steps_beside("VectorE", k, p, more):
                    step(*at)
                if k % (2 * EP) == WEIGH_LAG - 1:
                    dispatch(k // (2 * EP), p)

            def finish():
                low_part(UNITS - 1, PAIRS - 1)
                for k in range(SLOTS - WEIGH_LAG, SLOTS):
                    weigh(k, PAIRS - 1)
                step("back", 1, PAIRS - 1)

            turned(dve, front, slot, finish)


_INS = ["x", "L0_conv_w1", "L0_conv_gamma1", "L0_conv_beta1", "L0_conv_mean1", "L0_conv_var1",
        "L0_conv_w2", "L0_conv_gamma2", "L0_conv_beta2", "L0_conv_mean2", "L0_conv_var2",
        "L0_ffn_gate_w", "L0_ffn_gate_b", "L0_ffn_w1", "L0_ffn_w2", "L0_ffn_w3"]


def kernel(**inputs):
    import numpy as _np
    import concourse.bacc as _bacc
    from concourse import mybir as _mybir
    from concourse.bass_utils import run_bass_kernel_spmd as _run

    nc = _bacc.Bacc("TRN2", target_bir_lowering=False, num_devices=1)
    arrays, args = {}, []
    for name in _INS:
        a = _np.ascontiguousarray(inputs[name])
        arrays[f"in_{name}"] = a
        args.append(nc.dram_tensor(f"in_{name}", a.shape, _mybir.dt.from_np(a.dtype), kind="ExternalInput").ap())
    shape = arrays["in_x"].shape
    args.append(nc.dram_tensor("out_0", shape, _mybir.dt.float32, kind="ExternalOutput").ap())
    metaformer_kernel(nc, *args)
    r = _run(nc, [arrays], core_ids=[0])
    return r.results[0]["out_0"]
```
